# Optimizing a Trainium2 kernel written in Bass

```python
import numpy as np
import jax
import jax.numpy as jnp

def _softmax(x, axis=-1):
    return jax.nn.softmax(x, axis=axis)

def _gelu(x):
    return jax.nn.gelu(x, approximate=True)

def _silu(x):
    return jax.nn.silu(x)

def _sigmoid(x):
    return jax.nn.sigmoid(x)

def _layernorm(x, axis=-1, eps=1e-05):
    m = jnp.mean(x, axis=axis, keepdims=True)
    v = jnp.var(x, axis=axis, keepdims=True)
    return (x - m) / jnp.sqrt(v + eps)

def _scatter_add(tgt, idx, src, axis=0):
    return tgt.at[idx].add(src)

def _segment_sum(src, seg, n):
    return jax.ops.segment_sum(src, seg, n)
kernel_name = 'mk_hybrid_d1_jaxref_r8_0df43d'

def setup_inputs(seed: int=0):
    np.random.seed(seed)
    _w = jnp.asarray

    def _L0_attn_a_setup():
        import jax, jax.numpy as jnp
        import numpy as np
        SKIP_THRESHOLD = 0.3
        NUM_HEADS = 16
        TOP_K = 2

        def _layernorm(x, g, b, eps=1e-06):
            m = jnp.mean(x, axis=-1, keepdims=True)
            v = jnp.var(x, axis=-1, keepdims=True)
            return (x - m) * jax.lax.rsqrt(v + eps) * g + b

        def _silu(x):
            return x * jax.nn.sigmoid(x)

        def _causal_dwconv(x, w):
            k, S = (w.shape[0], x.shape[1])
            xp = jnp.pad(x, ((0, 0), (k - 1, 0), (0, 0)))
            return sum((xp[:, i:i + S, :] * w[i] for i in range(k)))

        def _same_dwconv(x, w):
            k, S = (w.shape[0], x.shape[1])
            pl = k // 2
            xp = jnp.pad(x, ((0, 0), (pl, k - 1 - pl), (0, 0)))
            return sum((xp[:, i:i + S, :] * w[i] for i in range(k)))

        def _mamba_block(x, w_in, conv_w, a_log, w_bc, w_dt, dt_bias, d_skip, w_out):
            B, S, D = x.shape
            d_inner = conv_w.shape[1]
            n = w_bc.shape[1] // 2
            xz = x @ w_in
            xc, z = (xz[..., :d_inner], xz[..., d_inner:])
            xc = _silu(_causal_dwconv(xc, conv_w))
            bc = xc @ w_bc
            Bt, Ct = (bc[..., :n], bc[..., n:])
            dt = jax.nn.softplus(xc * w_dt + dt_bias)
            A = -jnp.exp(a_log)

            def step(h, inp):
                xc_t, dt_t, B_t, C_t = inp
                decay = jnp.exp(dt_t * A)[..., None]
                h = decay * h + (dt_t * xc_t)[..., None] * B_t[:, None, :]
                y_t = jnp.einsum('bcn,bn->bc', h, C_t)
                return (h, y_t)
            h0 = jnp.zeros((B, d_inner, n), x.dtype)
            xs = (xc.transpose(1, 0, 2), dt.transpose(1, 0, 2), Bt.transpose(1, 0, 2), Ct.transpose(1, 0, 2))
            _, ys = jax.lax.scan(step, h0, xs)
            y = ys.transpose(1, 0, 2) + d_skip * xc
            return y * _silu(z) @ w_out

        def _timecrystal_block(x, theta, w, b):
            return jnp.cos(theta) * x + jnp.sin(theta) * jnp.tanh(x @ w + b)

        def _wlam_block(x, wq, wk, wv, wo, conv_w, nh):
            B, S, D = x.shape
            hd = D // nh
            inv = 0.7071067811865476
            xe, xo = (x[:, 0::2], x[:, 1::2])
            a = (xe + xo) * inv
            det = (xe - xo) * inv
            L = a.shape[1]
            q = (a @ wq).reshape(B, L, nh, hd)
            k = (a @ wk).reshape(B, L, nh, hd)
            v = (a @ wv).reshape(B, L, nh, hd)
            att = jnp.einsum('bqhd,bkhd->bhqk', q, k) * (1.0 / np.sqrt(hd))
            att = jax.nn.softmax(att, axis=-1)
            o = jnp.einsum('bhqk,bkhd->bqhd', att, v).reshape(B, L, D) @ wo
            xe2 = (o + det) * inv
            xo2 = (o - det) * inv
            y = jnp.stack([xe2, xo2], axis=2).reshape(B, S, D)
            return _same_dwconv(y, conv_w)

        def _moe_block(x, wg, w1, b1, w2, b2, top_k):
            B, S, D = x.shape
            E = wg.shape[1]
            xt = x.reshape(-1, D)
            logits = xt @ wg
            topv, topi = jax.lax.top_k(logits, top_k)
            w = jax.nn.softmax(topv, axis=-1)
            gates = (jax.nn.one_hot(topi, E, dtype=x.dtype) * w[..., None]).sum(axis=1)
            y = jnp.zeros_like(xt)
            for e in range(E):
                h = jax.nn.gelu(xt @ w1[e] + b1[e])
                y = y + gates[:, e:e + 1] * (h @ w2[e] + b2[e])
            return y.reshape(B, S, D)
        key = jax.random.key(seed)
        ks = jax.random.split(key, 20)
        B, S, D = (2, 256, 128)
        DI, N, CK = (2 * D, 64, 4)
        E, FF = (8, 512)
        NB = 4

        def rn(k, shape, scale=0.02):
            return jax.random.normal(k, shape, dtype=jnp.float32) * scale
        return {'hidden_states': jax.random.normal(ks[0], (B, S, D), jnp.float32), 'router_w': rn(ks[1], (D, NB)), 'router_b': jnp.zeros((NB,), jnp.float32), 'ln_g': jnp.ones((NB, D), jnp.float32), 'ln_b': jnp.zeros((NB, D), jnp.float32), 'm_win': rn(ks[2], (D, 2 * DI)), 'm_conv': rn(ks[3], (CK, DI), 0.1), 'm_alog': jnp.zeros((DI,), jnp.float32), 'm_wbc': rn(ks[4], (DI, 2 * N)), 'm_wdt': rn(ks[5], (DI,)), 'm_dtb': jnp.full((DI,), -1.0, jnp.float32), 'm_dskip': jnp.ones((DI,), jnp.float32), 'm_wout': rn(ks[6], (DI, D)), 'tc_theta': jnp.array(0.5, jnp.float32), 'tc_w': rn(ks[7], (D, D)), 'tc_b': jnp.zeros((D,), jnp.float32), 'w_q': rn(ks[8], (D, D)), 'w_k': rn(ks[9], (D, D)), 'w_v': rn(ks[10], (D, D)), 'w_o': rn(ks[11], (D, D)), 'wlam_conv': rn(ks[12], (4, D), 0.25), 'moe_wg': rn(ks[13], (D, E)), 'moe_w1': rn(ks[14], (E, D, FF)), 'moe_b1': jnp.zeros((E, FF), jnp.float32), 'moe_w2': rn(ks[15], (E, FF, D)), 'moe_b2': jnp.zeros((E, D), jnp.float32)}
    _L0_attn_a_in = _L0_attn_a_setup()

    def _L0_attn_b_setup():
        import jax, jax.numpy as jnp
        import numpy as np
        N, L, E = (4, 256, 128)
        HID, HEADS = (128, 16)
        key = jax.random.key(seed)
        ks = jax.random.split(key, 9)
        s = 1.0 / np.sqrt(E)
        return {'X_embed': jax.random.normal(ks[0], (N, L, E), dtype=jnp.float32), 'W_q': jax.random.normal(ks[1], (E, HID), dtype=jnp.float32) * s, 'b_q': jax.random.normal(ks[2], (HID,), dtype=jnp.float32) * 0.01, 'W_k': jax.random.normal(ks[3], (E, HID), dtype=jnp.float32) * s, 'b_k': jax.random.normal(ks[4], (HID,), dtype=jnp.float32) * 0.01, 'W_v': jax.random.normal(ks[5], (E, HID), dtype=jnp.float32) * s, 'b_v': jax.random.normal(ks[6], (HID,), dtype=jnp.float32) * 0.01, 'W_o': jax.random.normal(ks[7], (HID, HID), dtype=jnp.float32) * (1.0 / np.sqrt(HID)), 'b_o': jax.random.normal(ks[8], (HID,), dtype=jnp.float32) * 0.01}
    _L0_attn_b_in = _L0_attn_b_setup()

    def _L0_ffn_setup():
        import jax, jax.numpy as jnp
        import numpy as np
        N_HEAD = 16
        N_ACTIVE = 4
        D_MODEL = 128
        D_ATTN = 64
        B = 4
        S = 256
        key = jax.random.key(seed)
        ks = jax.random.split(key, 6)
        sc = 1.0 / np.sqrt(D_MODEL).astype(np.float32)
        return {'x': jax.random.normal(ks[0], (B, S, D_MODEL), jnp.float32), 'Wq': jax.random.normal(ks[1], (D_MODEL, N_HEAD * D_ATTN), jnp.float32) * sc, 'bq': jnp.zeros((N_HEAD * D_ATTN,), jnp.float32), 'Wk': jax.random.normal(ks[2], (D_MODEL, N_HEAD * D_ATTN), jnp.float32) * sc, 'bk': jnp.zeros((N_HEAD * D_ATTN,), jnp.float32), 'Wv': jax.random.normal(ks[3], (D_MODEL, N_HEAD * D_ATTN), jnp.float32) * sc, 'bv': jnp.zeros((N_HEAD * D_ATTN,), jnp.float32), 'Wr': jax.random.normal(ks[4], (D_MODEL, N_HEAD), jnp.float32) * sc, 'br': jnp.zeros((N_HEAD,), jnp.float32), 'Wo': jax.random.normal(ks[5], (N_ACTIVE * D_ATTN, D_MODEL), jnp.float32) * (1.0 / np.sqrt(N_ACTIVE * D_ATTN).astype(np.float32)), 'bo': jnp.zeros((D_MODEL,), jnp.float32)}
    _L0_ffn_in = _L0_ffn_setup()
    _d = {'L0_attn_a_hidden_states': _L0_attn_a_in['hidden_states'], 'L0_attn_a_router_w': _L0_attn_a_in['router_w'], 'L0_attn_a_router_b': _L0_attn_a_in['router_b'], 'L0_attn_a_ln_g': _L0_attn_a_in['ln_g'], 'L0_attn_a_ln_b': _L0_attn_a_in['ln_b'], 'L0_attn_a_m_win': _L0_attn_a_in['m_win'], 'L0_attn_a_m_conv': _L0_attn_a_in['m_conv'], 'L0_attn_a_m_alog': _L0_attn_a_in['m_alog'], 'L0_attn_a_m_wbc': _L0_attn_a_in['m_wbc'], 'L0_attn_a_m_wdt': _L0_attn_a_in['m_wdt'], 'L0_attn_a_m_dtb': _L0_attn_a_in['m_dtb'], 'L0_attn_a_m_dskip': _L0_attn_a_in['m_dskip'], 'L0_attn_a_m_wout': _L0_attn_a_in['m_wout'], 'L0_attn_a_tc_theta': _L0_attn_a_in['tc_theta'], 'L0_attn_a_tc_w': _L0_attn_a_in['tc_w'], 'L0_attn_a_tc_b': _L0_attn_a_in['tc_b'], 'L0_attn_a_w_q': _L0_attn_a_in['w_q'], 'L0_attn_a_w_k': _L0_attn_a_in['w_k'], 'L0_attn_a_w_v': _L0_attn_a_in['w_v'], 'L0_attn_a_w_o': _L0_attn_a_in['w_o'], 'L0_attn_a_wlam_conv': _L0_attn_a_in['wlam_conv'], 'L0_attn_a_moe_wg': _L0_attn_a_in['moe_wg'], 'L0_attn_a_moe_w1': _L0_attn_a_in['moe_w1'], 'L0_attn_a_moe_b1': _L0_attn_a_in['moe_b1'], 'L0_attn_a_moe_w2': _L0_attn_a_in['moe_w2'], 'L0_attn_a_moe_b2': _L0_attn_a_in['moe_b2'], 'L0_attn_b_W_q': _L0_attn_b_in['W_q'], 'L0_attn_b_b_q': _L0_attn_b_in['b_q'], 'L0_attn_b_W_k': _L0_attn_b_in['W_k'], 'L0_attn_b_b_k': _L0_attn_b_in['b_k'], 'L0_attn_b_W_v': _L0_attn_b_in['W_v'], 'L0_attn_b_b_v': _L0_attn_b_in['b_v'], 'L0_attn_b_W_o': _L0_attn_b_in['W_o'], 'L0_attn_b_b_o': _L0_attn_b_in['b_o'], 'L0_ffn_Wq': _L0_ffn_in['Wq'], 'L0_ffn_bq': _L0_ffn_in['bq'], 'L0_ffn_Wk': _L0_ffn_in['Wk'], 'L0_ffn_bk': _L0_ffn_in['bk'], 'L0_ffn_Wv': _L0_ffn_in['Wv'], 'L0_ffn_bv': _L0_ffn_in['bv'], 'L0_ffn_Wr': _L0_ffn_in['Wr'], 'L0_ffn_br': _L0_ffn_in['br'], 'L0_ffn_Wo': _L0_ffn_in['Wo'], 'L0_ffn_bo': _L0_ffn_in['bo']}
    _x0 = _d['L0_attn_a_hidden_states']
    _d['L0_attn_a_hidden_states'] = jax.random.normal(jax.random.fold_in(jax.random.key(seed), 1), (2, 2048, 128), dtype=_x0.dtype)
    del _x0
    return _d

def reference(L0_attn_a_hidden_states, L0_attn_a_router_w, L0_attn_a_router_b, L0_attn_a_ln_g, L0_attn_a_ln_b, L0_attn_a_m_win, L0_attn_a_m_conv, L0_attn_a_m_alog, L0_attn_a_m_wbc, L0_attn_a_m_wdt, L0_attn_a_m_dtb, L0_attn_a_m_dskip, L0_attn_a_m_wout, L0_attn_a_tc_theta, L0_attn_a_tc_w, L0_attn_a_tc_b, L0_attn_a_w_q, L0_attn_a_w_k, L0_attn_a_w_v, L0_attn_a_w_o, L0_attn_a_wlam_conv, L0_attn_a_moe_wg, L0_attn_a_moe_w1, L0_attn_a_moe_b1, L0_attn_a_moe_w2, L0_attn_a_moe_b2, L0_attn_b_W_q, L0_attn_b_b_q, L0_attn_b_W_k, L0_attn_b_b_k, L0_attn_b_W_v, L0_attn_b_b_v, L0_attn_b_W_o, L0_attn_b_b_o, L0_ffn_Wq, L0_ffn_bq, L0_ffn_Wk, L0_ffn_bk, L0_ffn_Wv, L0_ffn_bv, L0_ffn_Wr, L0_ffn_br, L0_ffn_Wo, L0_ffn_bo):

    def _L0_attn_a_ref(hidden_states, router_w, router_b, ln_g, ln_b, m_win, m_conv, m_alog, m_wbc, m_wdt, m_dtb, m_dskip, m_wout, tc_theta, tc_w, tc_b, w_q, w_k, w_v, w_o, wlam_conv, moe_wg, moe_w1, moe_b1, moe_w2, moe_b2):
        import jax, jax.numpy as jnp
        import numpy as np
        SKIP_THRESHOLD = 0.3
        NUM_HEADS = 16
        TOP_K = 2

        def _layernorm(x, g, b, eps=1e-06):
            m = jnp.mean(x, axis=-1, keepdims=True)
            v = jnp.var(x, axis=-1, keepdims=True)
            return (x - m) * jax.lax.rsqrt(v + eps) * g + b

        def _silu(x):
            return x * jax.nn.sigmoid(x)

        def _causal_dwconv(x, w):
            k, S = (w.shape[0], x.shape[1])
            xp = jnp.pad(x, ((0, 0), (k - 1, 0), (0, 0)))
            return sum((xp[:, i:i + S, :] * w[i] for i in range(k)))

        def _same_dwconv(x, w):
            k, S = (w.shape[0], x.shape[1])
            pl = k // 2
            xp = jnp.pad(x, ((0, 0), (pl, k - 1 - pl), (0, 0)))
            return sum((xp[:, i:i + S, :] * w[i] for i in range(k)))

        def _mamba_block(x, w_in, conv_w, a_log, w_bc, w_dt, dt_bias, d_skip, w_out):
            B, S, D = x.shape
            d_inner = conv_w.shape[1]
            n = w_bc.shape[1] // 2
            xz = x @ w_in
            xc, z = (xz[..., :d_inner], xz[..., d_inner:])
            xc = _silu(_causal_dwconv(xc, conv_w))
            bc = xc @ w_bc
            Bt, Ct = (bc[..., :n], bc[..., n:])
            dt = jax.nn.softplus(xc * w_dt + dt_bias)
            A = -jnp.exp(a_log)

            def step(h, inp):
                xc_t, dt_t, B_t, C_t = inp
                decay = jnp.exp(dt_t * A)[..., None]
                h = decay * h + (dt_t * xc_t)[..., None] * B_t[:, None, :]
                y_t = jnp.einsum('bcn,bn->bc', h, C_t)
                return (h, y_t)
            h0 = jnp.zeros((B, d_inner, n), x.dtype)
            xs = (xc.transpose(1, 0, 2), dt.transpose(1, 0, 2), Bt.transpose(1, 0, 2), Ct.transpose(1, 0, 2))
            _, ys = jax.lax.scan(step, h0, xs)
            y = ys.transpose(1, 0, 2) + d_skip * xc
            return y * _silu(z) @ w_out

        def _timecrystal_block(x, theta, w, b):
            return jnp.cos(theta) * x + jnp.sin(theta) * jnp.tanh(x @ w + b)

        def _wlam_block(x, wq, wk, wv, wo, conv_w, nh):
            B, S, D = x.shape
            hd = D // nh
            inv = 0.7071067811865476
            xe, xo = (x[:, 0::2], x[:, 1::2])
            a = (xe + xo) * inv
            det = (xe - xo) * inv
            L = a.shape[1]
            q = (a @ wq).reshape(B, L, nh, hd)
            k = (a @ wk).reshape(B, L, nh, hd)
            v = (a @ wv).reshape(B, L, nh, hd)
            att = jnp.einsum('bqhd,bkhd->bhqk', q, k) * (1.0 / np.sqrt(hd))
            att = jax.nn.softmax(att, axis=-1)
            o = jnp.einsum('bhqk,bkhd->bqhd', att, v).reshape(B, L, D) @ wo
            xe2 = (o + det) * inv
            xo2 = (o - det) * inv
            y = jnp.stack([xe2, xo2], axis=2).reshape(B, S, D)
            return _same_dwconv(y, conv_w)

        def _moe_block(x, wg, w1, b1, w2, b2, top_k):
            B, S, D = x.shape
            E = wg.shape[1]
            xt = x.reshape(-1, D)
            logits = xt @ wg
            topv, topi = jax.lax.top_k(logits, top_k)
            w = jax.nn.softmax(topv, axis=-1)
            gates = (jax.nn.one_hot(topi, E, dtype=x.dtype) * w[..., None]).sum(axis=1)
            y = jnp.zeros_like(xt)
            for e in range(E):
                h = jax.nn.gelu(xt @ w1[e] + b1[e])
                y = y + gates[:, e:e + 1] * (h @ w2[e] + b2[e])
            return y.reshape(B, S, D)
        h = hidden_states
        pooled = jnp.mean(h, axis=1)
        scores = jax.nn.sigmoid(pooled @ router_w + router_b)
        masks = (scores > SKIP_THRESHOLD).astype(h.dtype)
        h = h + masks[:, 0, None, None] * _mamba_block(_layernorm(h, ln_g[0], ln_b[0]), m_win, m_conv, m_alog, m_wbc, m_wdt, m_dtb, m_dskip, m_wout)
        h = h + masks[:, 1, None, None] * _timecrystal_block(_layernorm(h, ln_g[1], ln_b[1]), tc_theta, tc_w, tc_b)
        h = h + masks[:, 2, None, None] * _wlam_block(_layernorm(h, ln_g[2], ln_b[2]), w_q, w_k, w_v, w_o, wlam_conv, NUM_HEADS)
        h = h + masks[:, 3, None, None] * _moe_block(_layernorm(h, ln_g[3], ln_b[3]), moe_wg, moe_w1, moe_b1, moe_w2, moe_b2, TOP_K)
        return h

    def _L0_attn_b_ref(X_embed, W_q, b_q, W_k, b_k, W_v, b_v, W_o, b_o):
        import jax, jax.numpy as jnp
        import numpy as np
        N, L, E = (4, 256, 128)
        HID, HEADS = (128, 16)
        heads = HEADS
        n, l, _ = X_embed.shape
        hid = W_q.shape[1]
        d = hid // heads
        scale = 1.0 / np.sqrt(hid).astype(np.float32)
        Q = X_embed @ W_q + b_q
        K = X_embed @ W_k + b_k
        V = X_embed @ W_v + b_v
        Q = (Q * scale).reshape(n, heads, l, d)
        K = (K * scale).reshape(n, heads, l, d)
        V = V.reshape(n, heads, l, d)
        scores = jnp.einsum('neax,nebx->neab', Q, K)
        A = jax.nn.softmax(scores, axis=2)
        diag = jnp.diagonal(A, axis1=2, axis2=3)
        out = diag[..., None] * V
        out = out.reshape(n, l, hid)
        return out @ W_o + b_o

    def _L0_ffn_ref(x, Wq, bq, Wk, bk, Wv, bv, Wr, br, Wo, bo):
        import jax, jax.numpy as jnp
        import numpy as np
        N_HEAD = 16
        N_ACTIVE = 4
        D_MODEL = 128
        D_ATTN = 64
        B = 4
        S = 256
        b, s, _ = x.shape
        dist = jax.nn.softmax(jnp.mean(x @ Wr + br, axis=1), axis=-1)
        _, idx = jax.lax.top_k(dist, N_ACTIVE)
        idx = jnp.sort(idx, axis=-1)

        def proj(W, bias):
            return (x @ W + bias).reshape(b, s, N_HEAD, D_ATTN).transpose(0, 2, 1, 3)
        Q = proj(Wq, bq)
        K = proj(Wk, bk)
        V = proj(Wv, bv)
        gather = lambda t: jnp.take_along_axis(t, idx[:, :, None, None], axis=1)
        Qs, Ks, Vs = (gather(Q), gather(K), gather(V))
        scale = 1.0 / jnp.sqrt(jnp.asarray(D_ATTN, x.dtype))
        score = jax.nn.softmax(jnp.einsum('bhqd,bhkd->bhqk', Qs, Ks) * scale, axis=-1)
        O = jnp.einsum('bhqk,bhkd->bhqd', score, Vs)
        O = O.transpose(0, 2, 1, 3).reshape(b, s, N_ACTIVE * D_ATTN)
        return O @ Wo + bo
    x = L0_attn_a_hidden_states
    x = x + _L0_attn_a_ref(_layernorm(x, axis=-1), L0_attn_a_router_w, L0_attn_a_router_b, L0_attn_a_ln_g, L0_attn_a_ln_b, L0_attn_a_m_win, L0_attn_a_m_conv, L0_attn_a_m_alog, L0_attn_a_m_wbc, L0_attn_a_m_wdt, L0_attn_a_m_dtb, L0_attn_a_m_dskip, L0_attn_a_m_wout, L0_attn_a_tc_theta, L0_attn_a_tc_w, L0_attn_a_tc_b, L0_attn_a_w_q, L0_attn_a_w_k, L0_attn_a_w_v, L0_attn_a_w_o, L0_attn_a_wlam_conv, L0_attn_a_moe_wg, L0_attn_a_moe_w1, L0_attn_a_moe_b1, L0_attn_a_moe_w2, L0_attn_a_moe_b2)
    x = x + _L0_ffn_ref(_layernorm(x, axis=-1), L0_ffn_Wq, L0_ffn_bq, L0_ffn_Wk, L0_ffn_bk, L0_ffn_Wv, L0_ffn_bv, L0_ffn_Wr, L0_ffn_br, L0_ffn_Wo, L0_ffn_bo)
    x = x + _L0_attn_b_ref(_layernorm(x, axis=-1), L0_attn_b_W_q, L0_attn_b_b_q, L0_attn_b_W_k, L0_attn_b_b_k, L0_attn_b_W_v, L0_attn_b_b_v, L0_attn_b_W_o, L0_attn_b_b_o)
    x = x + _L0_ffn_ref(_layernorm(x, axis=-1), L0_ffn_Wq, L0_ffn_bq, L0_ffn_Wk, L0_ffn_bk, L0_ffn_Wv, L0_ffn_bv, L0_ffn_Wr, L0_ffn_br, L0_ffn_Wo, L0_ffn_bo)
    return x

_drawn_inputs = setup_inputs


def setup_inputs(seed=0):
    import zlib

    import numpy as np

    out = dict(_drawn_inputs(seed))
    spreads = {'L0_attn_a_router_b': (0.0, 0.1),
     'L0_attn_a_ln_g': (1.0, 0.2),
     'L0_attn_a_ln_b': (0.0, 0.1),
     'L0_attn_a_m_alog': (0.0, 0.8),
     'L0_attn_a_m_dtb': (-1.0, 0.6),
     'L0_attn_a_m_dskip': (1.0, 0.6),
     'L0_attn_a_tc_b': (0.0, 2.0),
     'L0_attn_a_moe_b1': (0.0, 2.0),
     'L0_attn_a_moe_b2': (0.0, 2.0),
     'L0_ffn_bq': (0.0, 2.0),
     'L0_ffn_bk': (0.0, 2.0),
     'L0_ffn_bv': (0.0, 2.0),
     'L0_ffn_br': (0.0, 0.8),
     'L0_ffn_bo': (0.0, 2.0)}
    factors = {'L0_attn_a_m_win': 8.0,
     'L0_attn_a_m_conv': 8.0,
     'L0_attn_a_m_wbc': 8.0,
     'L0_attn_a_m_wdt': 8.0,
     'L0_attn_a_m_wout': 8.0,
     'L0_attn_a_w_q': 64.0,
     'L0_attn_a_w_k': 64.0,
     'L0_attn_a_w_v': 64.0,
     'L0_attn_a_w_o': 64.0,
     'L0_attn_a_moe_w1': 32.784,
     'L0_attn_a_moe_w2': 29.8,
     'L0_attn_b_W_q': 64.0,
     'L0_attn_b_b_q': 200.0,
     'L0_attn_b_W_k': 64.0,
     'L0_attn_b_b_k': 200.0,
     'L0_attn_b_W_v': 64.0,
     'L0_attn_b_b_v': 200.0,
     'L0_attn_b_W_o': 64.0,
     'L0_attn_b_b_o': 200.0,
     'L0_ffn_Wr': 28.064,
     'L0_attn_a_tc_w': 42.667,
     'L0_attn_a_wlam_conv': 8.0,
     'L0_attn_a_moe_wg': 8.0,
     'L0_ffn_Wq': 8.0,
     'L0_ffn_Wk': 8.0,
     'L0_ffn_Wv': 8.0,
     'L0_ffn_Wo': 8.0}
    for name, (base, spread) in spreads.items():
        noise = np.random.default_rng([zlib.crc32(name.encode()), seed]).standard_normal(out[name].shape)
        drawn = base * np.exp(spread * noise) if base else spread * noise
        out[name] = jnp.asarray(drawn.astype(out[name].dtype))
    for name, factor in factors.items():
        out[name] = (out[name] * factor).astype(out[name].dtype)
    return out
```

```python
from contextlib import ExitStack

import numpy as np
import concourse.bass as bass
from concourse import mybir
from concourse.alu_op_type import AluOpType as ALU

F32, BF16, I32 = mybir.dt.float32, mybir.dt.bfloat16, mybir.dt.int32
ACT = mybir.ActivationFunctionType
X = mybir.AxisListType.X

P = 128
D = 128
BANK = 512
NEG_LOG = 7


class Engine:

    def __init__(self, queue, sem):
        self.q, self.sem, self.count, self.seen = queue, sem, 0, {}

    def op(self, ins):
        ins.then_inc(self.sem, 1)
        self.count += 1
        return (self.sem, self.count)

    def step(self, ins):
        point = self.op(ins)
        self.wait(point)
        return point

    def now(self):
        return (self.sem, self.count)

    def wait(self, *points):
        for p in points:
            if p is None or p[1] <= 0 or self.seen.get(p[0].name, 0) >= p[1]:
                continue
            self.q.wait_ge(p[0], p[1])
            self.seen[p[0].name] = p[1]


class Loads:

    def __init__(self, engine, sem):
        self.e, self.sem, self.count = engine, sem, 0

    def start(self, dst, src):
        self.e.q.dma_start(dst, src).then_inc(self.sem, 16)
        self.count += 16
        return (self.sem, self.count)

    def now(self):
        return (self.sem, self.count)


class Ring:

    def __init__(self, pe, groups):
        self.pe, self.groups, self.free, self.at = pe, groups, [None] * len(groups), 0

    def take(self):
        k = self.at
        self.at = (k + 1) % len(self.groups)
        self.pe.wait(self.free[k])
        return k, self.groups[k]

    def release(self, k, point):
        self.free[k] = point


def wide(ap, dim, n):
    shape = list(ap.shape)
    shape[dim] = n
    return ap.broadcast_to(shape)


def level_masks():
    s, t = np.arange(P)[:, None], np.arange(P)[None, :]
    sums, pairs = np.zeros((P, 9, P), np.float32), np.zeros((P, NEG_LOG, P), np.float32)
    for l in range(NEG_LOG):
        h = 1 << l
        same = (s // (2 * h)) == (t // (2 * h))
        s2, t2 = (s % (2 * h)) >= h, (t % (2 * h)) >= h
        sums[:, l] = same & ((~t2 & ~s2 & (s > t)) | (t2 & s2 & (s <= t)))
        pairs[:, l] = same & ~s2 & t2
    sums[:, 7] = s > t
    sums[:, 8] = s <= t
    return sums, pairs


def constants():
    sums, pairs = level_masks()
    h, o = np.arange(16)[:, None], np.arange(16)[None, :]
    before = (o < h).astype(np.float32).reshape(1, 256)
    return {
        "c_ident": np.eye(P, dtype=np.float32),
        "c_sums": sums,
        "c_pairs": pairs,
        "c_before": np.repeat(before, P, 0),
        "c_index": np.repeat(np.arange(16, dtype=np.float32)[None], P, 0),
        "c_before8": np.repeat((np.arange(8)[None] < np.arange(8)[:, None]).astype(np.float32).reshape(1, 64), P, 0),
    }


def build(nc, a, out, shape, phases=("H", "M", "T", "C", "D", "E", "F", "E2")):
    NB, S, _ = shape
    NT = S // P
    R = NB * NT
    ctx = ExitStack()
    with ctx:
        sem = lambda n: ctx.enter_context(nc.semaphore(n))
        PE, V, A, G = (Engine(q, sem(n)) for q, n in
                       ((nc.tensor, "pe_done"), (nc.vector, "dve_done"), (nc.scalar, "act_done"),
                        (nc.gpsimd, "pool_done")))
        SP = Engine(nc.sync, sem("sp_done"))
        engines = (PE, V, A, G, SP)
        loads = []

        def new_loads(name, engine=None):
            l = Loads(engine or SP, sem(name))
            loads.append(l)
            return l

        def barrier():
            points = [e.now() for e in engines] + [l.now() for l in loads]
            for e in engines:
                e.wait(*points)

        def sb(stack, name, shp, dt=F32):
            return stack.enter_context(nc.sbuf_tensor(name, shp, dt))

        psum = ctx.enter_context(nc.psum_tensor("psum", [P, 8, BANK], F32))
        bank = lambda k: psum[:, k, :]

        def bcast(ap, n):
            return wide(ap.rearrange("(o n) -> o n", o=1), 0, n)

        res = sb(ctx, "residual", [P, R, D])
        hid = sb(ctx, "hidden", [P, R, D])
        norm = sb(ctx, "normed", [P, NT, D])
        PAD = 4
        chans = sb(ctx, "normed_channels", [P, NB, PAD + S])
        ident = sb(ctx, "ident", [P, P])
        identb = sb(ctx, "ident_bf16", [P, P], BF16)
        stats = sb(ctx, "ln_stats", [P, NT, 6])
        mv = sb(ctx, "ln_mean_var", [P, NT, 2])
        rstd = sb(ctx, "ln_rstd", [P, NT])
        ones = sb(ctx, "ones", [P, P])
        mask = sb(ctx, "block_masks", [P, NB, 4])
        ln_g = sb(ctx, "ln_gains", [P, 4, D])
        ln_b = sb(ctx, "ln_biases", [P, 4, D])

        first = new_loads("first_loads")
        xt = a["hidden_states"].rearrange("b (i p) d -> p (b i) d", p=P)
        first.start(ident[:, :], a["c_ident"])
        for b in range(NB):
            first.start(res[:, b * NT:(b + 1) * NT, :], xt[:, b * NT:(b + 1) * NT, :])
        for j in range(4):
            first.start(ln_g[:, j, :], bcast(a["ln_g"][j, :], P))
            first.start(ln_b[:, j, :], bcast(a["ln_b"][j, :], P))
        for e in (PE, V, A, G):
            e.wait(first.now())
        V.op(nc.vector.memset(ones[:, :], 1.0))
        V.op(nc.vector.memset(chans[:, :, 0:PAD], 0.0))
        V.step(nc.vector.tensor_copy(identb[:, :], ident[:, :]))

        def layernorm(src, dst, b, eps, j=None):
            t0 = b * NT
            for i in range(NT):
                V.op(nc.vector.bn_stats(stats[:, i, :], src[:, t0 + i, :]))
            V.wait(V.now())
            for i in range(NT):
                V.op(nc.vector.bn_aggr(mv[:, i, :], stats[:, i, :]))
            V.wait(V.now())
            var = V.op(nc.vector.tensor_scalar(rstd[:, :], mv[:, :, 1], eps, None, ALU.add))
            A.wait(var)
            std = A.op(nc.scalar.activation(rstd[:, :], rstd[:, :], ACT.Sqrt))
            V.wait(std)
            V.step(nc.vector.reciprocal(rstd[:, :], rstd[:, :]))
            for i in range(NT):
                V.op(nc.vector.tensor_scalar(dst[:, i, :], src[:, t0 + i, :], mv[:, i, 0:1],
                                             rstd[:, i:i + 1], ALU.subtract, ALU.mult))
            if j is not None:
                V.wait(V.now())
                V.step(nc.vector.tensor_tensor(dst, dst, wide(ln_g[:, j:j + 1, :], 1, NT), ALU.mult))
                V.step(nc.vector.tensor_tensor(dst, dst, wide(ln_b[:, j:j + 1, :], 1, NT), ALU.add))
            return V.now()

        def to_channels(ring, src, ready, b, n=NT, dst=None, off=PAD):
            dst = chans[:, b, :] if dst is None else dst[:, :]
            PE.wait(ready)
            for g in range(n // 4):
                k, (bk,) = ring.take()
                for q in range(4):
                    last = nc.tensor.transpose(bank(bk)[:, q * P:(q + 1) * P], src[:, 4 * g + q, :], ident[:, :])
                done = PE.op(last)
                e = A if g % 2 else V
                e.wait(done)
                o = dst[:, off + BANK * g:off + BANK * (g + 1)]
                ring.release(k, A.op(nc.scalar.copy(o, bank(bk))) if g % 2 else
                             V.op(nc.vector.tensor_copy(o, bank(bk))))
            return (A.now(), V.now())

        def phase_H():
            with ExitStack() as st:
                pooled = sb(st, "pooled", [P, NB])
                pooled_all = sb(st, "pooled_all", [P, NB, P])
                router_w = sb(st, "router_w", [P, 4])
                router_b = sb(st, "router_b", [P, 4])
                z = sb(st, "router_z", [P, NB, 4])
                ld = new_loads("router_loads")
                ld.start(router_w[:, :], a["router_w"])
                ld.start(router_b[:, :], bcast(a["router_b"], P))
                ring = Ring(PE, [(k,) for k in range(8)])
                for b in range(NB):
                    ready = layernorm(res, hid[:, b * NT:(b + 1) * NT, :], b, 1e-5)
                    PE.wait(ready)
                    k, (bk,) = ring.take()
                    for i in range(NT):
                        last = nc.tensor.matmul(bank(bk)[:, 0:1], hid[:, b * NT + i, :], ones[:, 0:1],
                                                start=(i == 0), stop=(i == NT - 1))
                    V.wait(PE.op(last))
                    V.step(nc.vector.tensor_scalar(pooled[:, b:b + 1], bank(bk)[:, 0:1], 1.0 / S, None, ALU.mult))
                    pool = V.op(nc.vector.tensor_scalar(pooled_all[:, b, :], ones[:, :], pooled[:, b:b + 1], None, ALU.mult))
                    ring.release(k, V.now())
                    PE.wait(pool, ld.now())
                    k, (bk,) = ring.take()
                    done = PE.op(nc.tensor.matmul(bank(bk)[:, 0:4], pooled_all[:, b, :], router_w[:, :],
                                                  start=True, stop=True))
                    V.wait(done, ld.now())
                    s = V.op(nc.vector.tensor_tensor(z[:, b, :], bank(bk)[:, 0:4], router_b[:, :], ALU.add))
                    ring.release(k, s)
                    A.wait(s)
                    e = A.op(nc.scalar.activation(z[:, b, :], z[:, b, :], ACT.Exp, scale=-1.0))
                    V.wait(e)
                    V.step(nc.vector.tensor_scalar(z[:, b, :], z[:, b, :], 1.0, None, ALU.add))
                    V.step(nc.vector.reciprocal(z[:, b, :], z[:, b, :]))
                    V.step(nc.vector.tensor_scalar(mask[:, b, :], z[:, b, :], 0.3, None, ALU.is_gt))
                barrier()

        def phase_M():
            DI = a["m_conv"].shape[1]
            N = a["m_wbc"].shape[1] // 2
            C2 = DI // P
            CK = a["m_conv"].shape[0]
            with ExitStack() as st:
                win = sb(st, "m_win", [P, 2 * DI])
                taps = sb(st, "m_taps", [P, CK, DI])
                wbc = sb(st, "m_wbc", [P, C2, 2 * N])
                wout = sb(st, "m_wout", [P, C2, D])
                neg_a = sb(st, "m_neg_a", [P, DI])
                wdt = sb(st, "m_wdt", [P, DI])
                dtb = sb(st, "m_dtb", [P, DI])
                dskip = sb(st, "m_dskip", [P, DI])
                sums = sb(st, "level_sums", [P, 9, P])
                pairs = sb(st, "level_pairs", [P, NEG_LOG, P])
                ld = new_loads("mamba_loads")
                ld.start(win[:, :], a["m_win"])
                for c in range(CK):
                    ld.start(taps[:, c, :], bcast(a["m_conv"][c, :], P))
                ld.start(wbc[:, :, :], a["m_wbc"].rearrange("(k p) n -> p k n", p=P))
                ld.start(wout[:, :, :], a["m_wout"].rearrange("(k p) n -> p k n", p=P))
                for t, n in ((neg_a, "m_alog"), (wdt, "m_wdt"), (dtb, "m_dtb"), (dskip, "m_dskip")):
                    ld.start(t[:, :], bcast(a[n], P))
                ld.start(sums[:, :, :], a["c_sums"])
                ld.start(pairs[:, :, :], a["c_pairs"])
                V.wait(ld.now()); A.wait(ld.now()); G.wait(ld.now()); PE.wait(ld.now())
                for c in range(CK):
                    V.op(nc.vector.tensor_tensor(taps[:, c, :], taps[:, c, :], win[:, 0:DI], ALU.mult))
                taps_ready = V.now()
                neg = A.op(nc.scalar.activation(neg_a[:, :], neg_a[:, :], ACT.Exp))
                V.wait(neg)
                V.step(nc.vector.tensor_scalar(neg_a[:, :], neg_a[:, :], -1.0, None, ALU.mult))
                G.wait(V.now())

                xz = sb(st, "m_xz", [P, NT, 2 * DI])
                dta = sb(st, "m_dta", [P, NT, DI])
                dtx = sb(st, "m_dtx", [P, NT, DI])
                Q4 = 4
                xT = sb(st, "m_xT", [P, 2, C2, P])
                bctok = sb(st, "m_bc", [P, 3, 2 * N])
                bct = sb(st, "m_bcT", [N, 3, 2, P])
                gtt = sb(st, "m_gdiag", [P, 3, 1])
                gjunk = sb(st, "m_gjunk", [P, N])
                gm = sb(st, "m_pairs", [P, 3, NEG_LOG, P])
                dec = sb(st, "m_decay", [P, 2, 9, DI])
                total = sb(st, "m_total", [N, 2, DI])
                val = sb(st, "m_val", [P, 2, 8, DI])
                skip = sb(st, "m_skip", [P, 2, DI])
                zz = norm[:, :, :].rearrange("p (l c) n -> p l (c n)", l=8)
                yy = sb(st, "m_y", [P, DI])
                yT = sb(st, "m_yT", [P, C2, P])
                state = sb(st, "m_state", [N, DI])

                for b in range(NB):
                    ring = Ring(PE, [(k,) for k in range(8)])
                    ready = layernorm(hid, norm[:, :, :], b, 1e-6, 0)
                    done = to_channels(ring, norm, ready, b)
                    PE.wait(*done, taps_ready)
                    silu = []
                    for i in range(NT):
                        k, (bk,) = ring.take()
                        t0 = PAD + i * P
                        for c in range(CK):
                            nc.tensor.matmul(bank(bk)[:, 0:DI], chans[:, b, t0 + c - CK + 1:t0 + c - CK + 1 + P],
                                             taps[:, c, :], start=(c == 0), stop=(c == CK - 1))
                        p = PE.op(nc.tensor.matmul(bank(bk)[:, DI:2 * DI], chans[:, b, t0:t0 + P], win[:, DI:2 * DI],
                                                   start=True, stop=True))
                        A.wait(p)
                        silu.append(A.op(nc.scalar.activation(xz[:, i, :], bank(bk), ACT.Silu)))
                        ring.release(k, silu[-1])
                    wbuf = val[:, :, :, :].rearrange("p a l n -> p (a l) n")
                    row = lambda t: wide(t[:, :].rearrange("p (o n) -> p o n", o=1), 1, Q4)
                    groups = [slice(Q4 * q, Q4 * (q + 1)) for q in range(NT // Q4)]
                    vp, ep, wp, cp, lp = [], [], [], [], []
                    for q, g in enumerate(groups):
                        V.wait(silu[Q4 * (q + 1) - 1])
                        V.step(nc.vector.tensor_tensor(dtx[:, g, :], xz[:, g, 0:DI], row(wdt), ALU.mult))
                        vp.append(V.op(nc.vector.tensor_tensor(dtx[:, g, :], dtx[:, g, :], row(dtb), ALU.add)))
                    for q, g in enumerate(groups):
                        A.wait(vp[q])
                        ep.append(A.op(nc.scalar.activation(dta[:, g, :], dtx[:, g, :], ACT.Abs)))
                    for q, g in enumerate(groups):
                        A.wait(ep[q])
                        ep[q] = A.op(nc.scalar.activation(dta[:, g, :], dta[:, g, :], ACT.Exp, scale=-1.0))
                    for q, g in enumerate(groups):
                        V.wait(ep[q])
                        wp.append(V.op(nc.vector.tensor_scalar(wbuf[:, g, :], dta[:, g, :], 1.0, None, ALU.add)))
                    for q, g in enumerate(groups):
                        V.wait(wp[q])
                        cp.append(V.op(nc.vector.scalar_tensor_tensor(dta[:, g, :], wbuf[:, g, :], 1.0, dta[:, g, :], ALU.subtract, ALU.subtract)))
                    for q, g in enumerate(groups):
                        A.wait(cp[q])
                        lp.append(A.op(nc.scalar.activation(wbuf[:, g, :], wbuf[:, g, :], ACT.Ln)))
                    for q, g in enumerate(groups):
                        V.wait(lp[q])
                        V.step(nc.vector.tensor_tensor(wbuf[:, g, :], wbuf[:, g, :], dta[:, g, :], ALU.subtract))
                        p = V.op(nc.vector.scalar_tensor_tensor(wbuf[:, g, :], dtx[:, g, :], 0.0, wbuf[:, g, :], ALU.max, ALU.add))
                        G.wait(p)
                        G.op(nc.gpsimd.tensor_tensor(dta[:, g, :], wbuf[:, g, :], row(neg_a), ALU.mult))
                        G.op(nc.gpsimd.tensor_tensor(dtx[:, g, :], wbuf[:, g, :], xz[:, g, 0:DI], ALU.mult))
                    barrier()
                    V.step(nc.vector.memset(state[:, :], 0.0))

                    misc = Ring(PE, [(0,), (1,)])
                    dring = Ring(PE, [(2,), (3,)])
                    yfree = [None]
                    pt = {}

                    def chunk_front(i, j):
                        s = i % 2
                        kd, (bd,) = dring.take()
                        for h in range(2):
                            if 2 * j + h < 9:
                                last = nc.tensor.matmul(bank(bd)[:, h * DI:(h + 1) * DI], sums[:, 2 * j + h, :], dta[:, i, :],
                                                        start=True, stop=True)
                            else:
                                last = nc.tensor.matmul(bank(bd)[0:N, h * DI:(h + 1) * DI], ones[:, 0:N], dta[:, i, :],
                                                        start=True, stop=True)
                        A.wait(PE.op(last), pt.get(("z_read", i - 2)), pt.get(("state", i - 2)))
                        if j < 4:
                            p = A.op(nc.scalar.activation(dec[:, s, 2 * j:2 * j + 2, :],
                                                          bank(bd).rearrange("p (l n) -> p l n", l=2), ACT.Exp))
                            G.wait(p, pt.get(("pe_back", i - 2)))
                            pt["val", i] = G.op(nc.gpsimd.tensor_tensor(val[:, s, 2 * j:2 * j + 2, :], dec[:, s, 2 * j:2 * j + 2, :],
                                                                        wide(dtx[:, i:i + 1, :], 1, 2), ALU.mult))
                        else:
                            A.op(nc.scalar.activation(dec[:, s, 8, :], bank(bd)[:, 0:DI], ACT.Exp))
                            p = A.op(nc.scalar.activation(total[:, s, :], bank(bd)[0:N, DI:2 * DI], ACT.Exp))
                            pt["decays", i] = p
                            G.wait(pt.get(("y_read", i - 2)))
                            pt["skip", i] = G.op(nc.gpsimd.tensor_tensor(skip[:, s, :], xz[:, i, 0:DI], dskip[:, :], ALU.mult))
                        dring.release(kd, p)

                    def chunk_turn(i):
                        k, (bk,) = misc.take()
                        for c in range(C2):
                            last = nc.tensor.transpose(bank(bk)[:, c * P:(c + 1) * P], xz[:, i, c * P:(c + 1) * P], ident[:, :])
                        A.wait(PE.op(last), pt.get(("bc_made", i - 2)))
                        pt["xT", i] = A.op(nc.scalar.copy(xT[:, i % 2], bank(bk)[:, 0:C2 * P].rearrange("p (c t) -> p c t", c=C2)))
                        misc.release(k, pt["xT", i])

                    def chunk_bc(i):
                        s = i % 3
                        PE.wait(pt["xT", i])
                        k, (bk,) = misc.take()
                        for c in range(C2):
                            nc.tensor.matmul(bank(bk)[:, 0:2 * N], xT[:, i % 2, c, :], wbc[:, c, :], start=(c == 0), stop=(c == C2 - 1))
                        for h in range(2):
                            for c in range(C2):
                                last = nc.tensor.matmul(bank(bk)[0:N, (1 + h) * P:(2 + h) * P], wbc[:, c, h * N:(h + 1) * N],
                                                        xT[:, i % 2, c, :], start=(c == 0), stop=(c == C2 - 1))
                        pt["bc_made", i] = PE.op(last)
                        A.wait(pt["bc_made", i], pt.get(("pe_back", i - 3)), pt.get(("bc_read", i - 3)))
                        A.op(nc.scalar.copy(bctok[:, s, :], bank(bk)[:, 0:2 * N]))
                        pt["bc", i] = A.op(nc.scalar.copy(bct[:, s], bank(bk)[0:N, P:3 * P].rearrange("p (c t) -> p c t", c=2)))
                        misc.release(k, pt["bc", i])

                    def chunk_pairs(i):
                        s = i % 3
                        PE.wait(pt["bc", i])
                        k, (bk,) = misc.take()
                        gp = PE.op(nc.tensor.matmul(bank(bk)[:, 0:P], bct[:, s, 0, :], bct[:, s, 1, :], start=True, stop=True))
                        V.wait(gp, pt.get(("pe_back", i - 3)))
                        p = V.op(nc.vector.tensor_tensor(gm[:, s], wide(bank(bk)[:, 0:P].rearrange("p (o n) -> p o n", o=1), 1, NEG_LOG),
                                                         pairs[:, :, :], ALU.mult))
                        misc.release(k, p)
                        pt["gm", i] = p
                        V.wait(pt["bc", i], pt.get(("bc_read", i - 1)))
                        pt["bc_read", i] = V.op(nc.vector.tensor_tensor_reduce(gjunk[:, :], bctok[:, s, 0:N], bctok[:, s, N:2 * N], 1.0, 0.0,
                                                                               ALU.mult, ALU.add, gtt[:, s, :]))

                    def chunk_mix(i):
                        s, r = i % 2, i % 3
                        PE.wait(pt["val", i], pt["gm", i], yfree[0], pt.get(("state", i - 1)))
                        for l in range(NEG_LOG):
                            nc.tensor.matmul(bank(4 + l // 2)[:, (l % 2) * DI:(l % 2 + 1) * DI], gm[:, r, l, :], val[:, s, l, :],
                                             start=True, stop=True)
                        yp = PE.op(nc.tensor.matmul(bank(7)[:, DI:2 * DI], bct[:, r, 1, :], state[:, :], start=True, stop=True))
                        k, (bk,) = misc.take()
                        hp = PE.op(nc.tensor.matmul(bank(bk)[0:N, 0:DI], bctok[:, r, 0:N], val[:, s, 7, :], start=True, stop=True))
                        pt["pe_back", i] = hp
                        V.wait(yp, pt["decays", i], pt.get(("y_read", i - 1)))
                        V.op(nc.vector.tensor_tensor(zz[:, 0:7, :], psum[:, 4:8, :].rearrange("p b (l n) -> p (b l) n", l=2)[:, 0:7, :],
                                                     dec[:, s, 0:7, :], ALU.mult))
                        V.op(nc.vector.tensor_tensor(zz[:, 7, :], bank(7)[:, DI:2 * DI], dec[:, s, 8, :], ALU.mult))
                        yfree[0] = pt["z_read", i] = V.now()
                        V.step(nc.vector.tensor_tensor(state[:, :], state[:, :], total[:, s, :], ALU.mult))
                        V.wait(hp)
                        p = V.op(nc.vector.tensor_tensor(state[:, :], state[:, :], bank(bk)[0:N, 0:DI], ALU.add))
                        pt["state", i] = p
                        misc.release(k, p)
                        V.wait(pt["z_read", i], pt.get(("y_turned", i - 1)))
                        V.op(nc.vector.tensor_reduce(yy[:, :], zz[:, :, :].rearrange("p l n -> p n l"), X, ALU.add))
                        V.wait(pt["skip", i])
                        V.step(nc.vector.scalar_tensor_tensor(skip[:, s, :], dtx[:, i, :], gtt[:, r, :], skip[:, s, :], ALU.mult, ALU.add))
                        V.step(nc.vector.tensor_tensor(yy[:, :], yy[:, :], skip[:, s, :], ALU.add))
                        pt["y_read", i] = V.step(nc.vector.tensor_tensor(yy[:, :], yy[:, :], xz[:, i, DI:2 * DI], ALU.mult))

                    def chunk_out(i):
                        PE.wait(pt["y_read", i])
                        k, (bk,) = misc.take()
                        for c in range(C2):
                            last = nc.tensor.transpose(bank(bk)[:, c * P:(c + 1) * P], yy[:, c * P:(c + 1) * P], ident[:, :])
                        tp = PE.op(last)
                        pt["y_turned", i] = tp
                        A.wait(tp, pt.get(("yT_read", i - 1)))
                        yr = A.op(nc.scalar.copy(yT[:, :, :], bank(bk)[:, 0:C2 * P].rearrange("p (c t) -> p c t", c=C2)))
                        misc.release(k, yr)
                        PE.wait(yr)
                        k, (bk,) = misc.take()
                        for c in range(C2):
                            last = nc.tensor.matmul(bank(bk)[:, 0:D], yT[:, c, :], wout[:, c, :], start=(c == 0), stop=(c == C2 - 1))
                        op = PE.op(last)
                        pt["yT_read", i] = op
                        V.wait(op)
                        h = hid[:, b * NT + i, :]
                        p = V.op(nc.vector.scalar_tensor_tensor(h, bank(bk)[:, 0:D], mask[:, b, 0:1], h, ALU.mult, ALU.add))
                        misc.release(k, p)

                    for i in range(2):
                        chunk_turn(i)
                        chunk_bc(i)
                        chunk_pairs(i)
                    for j in range(5):
                        chunk_front(0, j)
                    for i in range(NT):
                        chunk_mix(i)
                        for j in range(5):
                            if i + 1 < NT:
                                chunk_front(i + 1, j)
                            if i + 2 < NT and j == 0:
                                chunk_turn(i + 2)
                            if i + 2 < NT and j == 3:
                                chunk_bc(i + 2)
                        if i + 2 < NT:
                            chunk_pairs(i + 2)
                        chunk_out(i)
                    barrier()

        def phase_T():
            with ExitStack() as st:
                w = sb(st, "tc_w", [P, D])
                bias = sb(st, "tc_b", [1, D])
                th = sb(st, "tc_theta", [P, 1])
                turn = sb(st, "tc_turn", [P, 1])
                cs = sb(st, "tc_cos_sin", [P, 2])
                tanh = sb(st, "tc_tanh", [P, NT, D])
                mixed = sb(st, "tc_mixed", [P, NT, D])
                ld = new_loads("tc_loads")
                ld.start(w[:, :], a["tc_w"])
                ld.start(bias[:, :], a["tc_b"].rearrange("(o n) -> o n", o=1))
                ld.start(th[:, :], wide(a["tc_theta"].rearrange("(o n) -> o n", o=1), 0, P))
                V.wait(ld.now()); PE.wait(ld.now())
                BIG = float(1.5 * 2 ** 23)
                V.step(nc.vector.tensor_scalar(turn[:, :], th[:, :], float(1 / (2 * np.pi)), BIG, ALU.mult, ALU.add))
                V.step(nc.vector.tensor_scalar(turn[:, :], turn[:, :], BIG, None, ALU.subtract))
                tau_hi = float(np.float32(6.28125))
                tau_lo = float(2 * np.pi - 6.28125)
                V.step(nc.vector.scalar_tensor_tensor(th[:, :], turn[:, :], -tau_hi, th[:, :], ALU.mult, ALU.add))
                V.step(nc.vector.scalar_tensor_tensor(th[:, :], turn[:, :], -tau_lo, th[:, :], ALU.mult, ALU.add))
                V.step(nc.vector.tensor_scalar(th[:, :], th[:, :], float(np.float32(np.pi)), -float(np.float32(np.pi)), ALU.min, ALU.max))
                V.step(nc.vector.scalar_tensor_tensor(turn[:, :], th[:, :], -1.0, th[:, :], ALU.mult, ALU.max))
                V.step(nc.vector.tensor_scalar(turn[:, :], turn[:, :], -1.0, float(np.pi / 2), ALU.mult, ALU.add))
                A.wait(V.now())
                A.op(nc.scalar.activation(cs[:, 0:1], turn[:, :], ACT.Sin))
                A.op(nc.scalar.activation(cs[:, 1:2], th[:, :], ACT.Sin))
                V.wait(A.now())
                for b in range(NB):
                    ring = Ring(PE, [(k,) for k in range(8)])
                    done = to_channels(ring, norm, layernorm(hid, norm[:, :, :], b, 1e-6, 1), b)
                    PE.wait(*done)
                    for g in range(NT // 4):
                        k, (bk,) = ring.take()
                        for q in range(4):
                            o = bank(bk)[:, q * D:(q + 1) * D]
                            nc.tensor.matmul(o, chans[:, b, PAD + (4 * g + q) * P:PAD + (4 * g + q + 1) * P], w[:, :], start=True, stop=False)
                            last = nc.tensor.matmul(o, ones[0:1, :], bias[:, :], start=False, stop=True)
                        A.wait(PE.op(last))
                        p = A.op(nc.scalar.activation(tanh[:, 4 * g:4 * g + 4, :], bank(bk).rearrange("p (q n) -> p q n", q=4), ACT.Tanh))
                        ring.release(k, p)
                    V.step(nc.vector.tensor_scalar(mixed[:, :, :], norm[:, :, :], cs[:, 0:1], None, ALU.mult))
                    V.wait(A.now())
                    V.step(nc.vector.scalar_tensor_tensor(mixed[:, :, :], tanh[:, :, :], cs[:, 1:2], mixed[:, :, :], ALU.mult, ALU.add))
                    h = hid[:, b * NT:(b + 1) * NT, :]
                    V.step(nc.vector.scalar_tensor_tensor(h, mixed[:, :, :], mask[:, b, 1:2], h, ALU.mult, ALU.add))
                    barrier()

        NG, HD, NH, ROWS = 9, 8, 16, 96

        def phase_C():
            B2 = S // 2
            CT = B2 // P
            HB = NH // 4
            with ExitStack() as st:
                wqkv = sb(st, "w_qkv", [P, 3 * D])
                wo = sb(st, "w_o", [P, D])
                cw = sb(st, "wlam_conv", [P, 4])
                ld = new_loads("wlam_loads")
                for j, n in enumerate(("w_q", "w_k", "w_v")):
                    ld.start(wqkv[:, j * D:(j + 1) * D], a[n])
                ld.start(wo[:, :], a["w_o"])
                with nc.allow_non_contiguous_dma("4 taps a channel"):
                    ld.start(cw[:, :], a["wlam_conv"].rearrange("k d -> d k"))
                chs = sb(st, "wl_scaled", [P, S])
                aT = sb(st, "wl_sum", [P, B2])
                dT = sb(st, "wl_diff", [P, B2])
                qf = sb(st, "wl_q", [P, 2, 2 * D])
                pr = [sb(st, f"wl_part{n}", [P, 2, 2 * D], F32 if n == 0 else BF16) for n in range(3)]
                uq = sb(st, "wl_q_rows", [P, CT, NH, ROWS], BF16)
                uk = sb(st, "wl_k_rows", [P, CT, NH, ROWS], BF16)
                qT = sb(st, "wl_qT", [ROWS, 4, B2], BF16)
                kT = sb(st, "wl_kT", [ROWS, 4, B2], BF16)
                vp = sb(st, "wl_v", [P, CT, NH, 32])
                negm = sb(st, "wl_negmax", [P, CT, NH])
                mrest = sb(st, "wl_negmax_rest", [P, CT, NH])
                pe_ = sb(st, "wl_p", [P, 3, 2 * BANK])
                oc = sb(st, "wl_oT", [P, 2 * BANK])
                rr = sb(st, "wl_recip", [P, CT, 4])
                otok = sb(st, "wl_o", [P, CT, D])
                oT = sb(st, "wl_oT2", [P, B2])
                yp = sb(st, "wl_y", [P, S + 4])
                cv = sb(st, "wl_cv", [P, S])
                for e in (PE, V, A, G):
                    e.wait(ld.now())
                V.op(nc.vector.memset(vp[:, :, :, :], 0.0))
                V.op(nc.vector.memset(yp[:, :], 0.0))
                G.op(nc.gpsimd.memset(uq[:, :, :, NG * HD:ROWS], 0.0))
                G.op(nc.gpsimd.memset(uk[:, :, :, NG * HD:ROWS], 0.0))
                V.wait(V.now()); G.wait(G.now())
                V.op(nc.vector.memset(vp[:, :, :, HD:HD + 1], 1.0))
                G.op(nc.gpsimd.memset(uk[:, :, :, NG * HD:NG * HD + 3], 1.0))
                for b in range(NB):
                    ring = Ring(PE, [(k,) for k in range(8)])
                    done = to_channels(ring, norm, layernorm(hid, norm[:, :, :], b, 1e-6, 2), b)
                    V.wait(*done)
                    INV = 0.7071067811865476
                    V.step(nc.vector.tensor_scalar(chs[:, :], chans[:, b, PAD:PAD + S], INV, None, ALU.mult))
                    eo = chs[:, :].rearrange("p (t e) -> p t e", e=2)
                    V.op(nc.vector.tensor_tensor(aT[:, :], eo[:, :, 0], eo[:, :, 1], ALU.add))
                    PE.wait(V.now())
                    V.op(nc.vector.tensor_tensor(dT[:, :], eo[:, :, 0], eo[:, :, 1], ALU.subtract))
                    used = [None, None]
                    for i in range(CT):
                        s = i % 2
                        k, (bk,) = ring.take()
                        A.wait(PE.op(nc.tensor.matmul(bank(bk)[:, 0:3 * D], aT[:, i * P:(i + 1) * P], wqkv[:, :], start=True, stop=True)), used[s])
                        A.op(nc.scalar.copy(qf[:, s, :], bank(bk)[:, 0:2 * D]))
                        p = A.op(nc.scalar.copy(vp[:, i, :, 0:HD], bank(bk)[:, 2 * D:3 * D].rearrange("p (h x) -> p h x", x=HD)))
                        ring.release(k, p)
                        split3(qf[:, s, :], pr[0][:, s, :], pr[1][:, s, :], pr[2][:, s, :], p,
                               [(uq[:, i], 0, True), (uk[:, i], D, False)])
                        used[s] = used_all()
                    if b:
                        G.op(nc.gpsimd.memset(uq[:, :, :, NG * HD:NG * HD + 3], 0.0))
                    barrier()
                    tr = Ring(PE, [(0,), (1,)])
                    sr = Ring(PE, [(2, 3), (4, 5), (6, 7)])
                    rows_done = [None, None]
                    for h in range(NH):
                        s = h % 4
                        PE.wait(G.now(), V.now() if h == 0 else None)
                        head_rows(tr, uq, qT, h, s, CT, rows_done)
                        pts = head_rows(tr, uk, kT, h, s, CT, rows_done)
                        PE.wait(*pts)
                        for i in range(CT):
                            k, bks = sr.take()
                            for j in range(B2 // BANK):
                                last = nc.tensor.matmul(bank(bks[j]), qT[:, s, i * P:(i + 1) * P], kT[:, s, j * BANK:(j + 1) * BANK],
                                                        start=True, stop=True)
                            V.wait(PE.op(last))
                            p = V.op(nc.vector.tensor_reduce(negm[:, i, h:h + 1], psum[:, bks[0]:bks[0] + 2, :].rearrange("p b n -> p (b n)"),
                                                             X, ALU.max, negate=True))
                            sr.release(k, p)
                    barrier()
                    mr = NG * HD
                    V.step(nc.vector.tensor_copy(uq[:, :, :, mr], negm[:, :, :]))
                    V.step(nc.vector.tensor_tensor(mrest[:, :, :], negm[:, :, :], uq[:, :, :, mr], ALU.subtract))
                    V.step(nc.vector.tensor_copy(uq[:, :, :, mr + 1], mrest[:, :, :]))
                    V.step(nc.vector.tensor_tensor(mrest[:, :, :], mrest[:, :, :], uq[:, :, :, mr + 1], ALU.subtract))
                    V.step(nc.vector.tensor_copy(uq[:, :, :, mr + 2], mrest[:, :, :]))
                    PE.wait(V.now())
                    tr = Ring(PE, [(0,), (1,)])
                    sr = Ring(PE, [(2, 3), (4, 5)])
                    orr = Ring(PE, [(6, 7)])
                    SC = 1.0 / float(np.sqrt(HD))
                    pfree = [None] * 3
                    u = 0
                    for hg in range(HB):
                        for hh in range(4):
                            head_rows(tr, uq, qT, 4 * hg + hh, hh, CT, rows_done)
                            pts = head_rows(tr, uk, kT, 4 * hg + hh, hh, CT, rows_done)
                        PE.wait(*pts)
                        ko, (o0, o1) = orr.take()
                        pend = []

                        def av(item):
                            kt, hh, slot, ep = item
                            PE.wait(ep)
                            for j in range(2):
                                last = nc.tensor.matmul(bank((o0, o1)[j])[32 * hh:32 * hh + 32, :], vp[:, kt, 4 * hg + hh, :],
                                                        pe_[:, slot, j * BANK:(j + 1) * BANK], start=(kt == 0), stop=(kt == CT - 1),
                                                        skip_group_check=True, tile_position=(0, 32 * hh))
                            return PE.op(last)
                        for kt in range(CT):
                            for hh in range(4):
                                k, bks = sr.take()
                                for j in range(2):
                                    last = nc.tensor.matmul(bank(bks[j]), kT[:, hh, kt * P:(kt + 1) * P], qT[:, hh, j * BANK:(j + 1) * BANK],
                                                            start=True, stop=True)
                                slot = u % 3
                                u += 1
                                A.wait(PE.op(last), pfree[slot])
                                p = A.op(nc.scalar.activation(pe_[:, slot, :], psum[:, bks[0]:bks[0] + 2, :].rearrange("p b n -> p (b n)"),
                                                              ACT.Exp, scale=SC))
                                sr.release(k, p)
                                pend.append((kt, hh, slot, p))
                                if len(pend) > 1:
                                    it = pend.pop(0)
                                    pfree[it[2]] = av(it)
                        while pend:
                            it = pend.pop(0)
                            pfree[it[2]] = av(it)
                        V.wait(PE.now())
                        V.step(nc.vector.tensor_copy(oc[:, :], psum[:, o0:o0 + 2, :].rearrange("p b n -> p (b n)")))
                        orr.release(ko, V.now())
                        PE.wait(V.now())
                        for g in range(CT // 4):
                            k, (bk,) = tr.take()
                            for q in range(4):
                                t = 4 * g + q
                                last = nc.tensor.transpose(bank(bk)[:, q * P:(q + 1) * P], oc[:, t * P:(t + 1) * P], ident[:, :])
                            V.wait(PE.op(last))
                            v4 = bank(bk).rearrange("p (q h x) -> p q h x", q=4, h=4)
                            V.step(nc.vector.reciprocal(rr[:, 4 * g:4 * g + 4, :], v4[:, :, :, HD]))
                            for q in range(4):
                                p = V.op(nc.vector.tensor_tensor(
                                    otok[:, 4 * g + q, 32 * hg:32 * hg + 32].rearrange("p (h x) -> p h x", x=HD), v4[:, q, :, 0:HD],
                                    wide(rr[:, 4 * g + q, :].rearrange("p (h o) -> p h o", o=1), 2, HD), ALU.mult))
                            tr.release(k, p)
                    barrier()
                    ring = Ring(PE, [(k,) for k in range(8)])
                    done = to_channels(ring, otok, V.now(), b, CT, oT, 0)
                    PE.wait(*done)
                    yv = yp[:, 2:2 + S].rearrange("p (t e) -> p t e", e=2)
                    for j in range(B2 // BANK):
                        k, (bk,) = ring.take()
                        V.wait(PE.op(nc.tensor.matmul(bank(bk), wo[:, :], oT[:, j * BANK:(j + 1) * BANK], start=True, stop=True)))
                        dj = dT[:, j * BANK:(j + 1) * BANK]
                        V.op(nc.vector.tensor_tensor(yv[:, j * BANK:(j + 1) * BANK, 0], bank(bk), dj, ALU.add))
                        p = V.op(nc.vector.tensor_tensor(yv[:, j * BANK:(j + 1) * BANK, 1], bank(bk), dj, ALU.subtract))
                        ring.release(k, p)
                    V.wait(V.now())
                    V.step(nc.vector.tensor_scalar(yp[:, 2:2 + S], yp[:, 2:2 + S], INV, None, ALU.mult))
                    V.step(nc.vector.tensor_scalar(cv[:, :], yp[:, 0:S], cw[:, 0:1], None, ALU.mult))
                    for c in range(1, 4):
                        V.step(nc.vector.scalar_tensor_tensor(cv[:, :], yp[:, c:c + S], cw[:, c:c + 1], cv[:, :], ALU.mult, ALU.add))
                    PE.wait(V.now())
                    for g in range(NT // 4):
                        k, (bk,) = ring.take()
                        for q in range(4):
                            t = 4 * g + q
                            last = nc.tensor.transpose(bank(bk)[:, q * P:(q + 1) * P], cv[:, t * P:(t + 1) * P], ident[:, :])
                        V.wait(PE.op(last))
                        h = hid[:, b * NT + 4 * g:b * NT + 4 * g + 4, :]
                        p = V.op(nc.vector.scalar_tensor_tensor(h, bank(bk).rearrange("p (q n) -> p q n", q=4), mask[:, b, 2:3], h,
                                                                ALU.mult, ALU.add))
                        ring.release(k, p)
                    barrier()

        def split3(src, rest, hi, mid, ready, targets):
            def spread(g, part, point):
                for e, (dst, c0, q_side) in enumerate(targets):
                    rows = dst[:, :, 0:NG * HD].rearrange("p h (i j x) -> p h i j x", i=3, j=3)
                    src8 = part[:, c0:c0 + D].rearrange("p (h x) -> p h x", x=HD)
                    for c in range(3):
                        o = rows[:, :, g, c, :] if q_side else rows[:, :, c, g, :]
                        if c == 0:
                            A.wait(point)
                            A.op(nc.scalar.copy(o, src8))
                        elif c == 1 or e == 0:
                            G.wait(point)
                            G.op(nc.gpsimd.tensor_copy(o, src8))
                        else:
                            V.wait(point)
                            V.op(nc.vector.tensor_copy(o, src8))
            V.wait(ready)
            p = V.step(nc.vector.tensor_copy(hi, src))
            spread(0, hi, p)
            V.step(nc.vector.tensor_tensor(rest, src, hi, ALU.subtract))
            p = V.step(nc.vector.tensor_copy(mid, rest))
            spread(1, mid, p)
            V.wait(G.now(), A.now())
            p = V.step(nc.vector.tensor_tensor(hi, rest, mid, ALU.subtract))
            spread(2, hi, p)

        def used_all():
            V.wait(G.now())
            V.wait(A.now())
            A.wait(V.now())
            return None

        def head_rows(ring, u, dst, h, s, n, done):
            pts = []
            for g in range(n // 8 if n >= 8 else 1):
                k, (bk,) = ring.take()
                bv = psum[0:ROWS, bk, :].bitcast(BF16)
                for q in range(8):
                    last = nc.tensor.transpose(bv[:, q * P:(q + 1) * P], u[:, 8 * g + q, h, :], identb[:, :])
                p = PE.op(last)
                A.wait(p)
                p = A.op(nc.scalar.copy(dst[:, s, g * 8 * P:(g + 1) * 8 * P], bv))
                ring.release(k, p)
                pts.append(p)
            return pts

        def phase_D():
            E_, _, FF = a["moe_w1"].shape
            FT = FF // P
            with ExitStack() as st:
                w1 = sb(st, "moe_w1", [P, E_, FF])
                w2 = sb(st, "moe_w2", [P, E_ * FT, D])
                b1 = sb(st, "moe_b1", [P, E_ * FT])
                b2 = sb(st, "moe_b2", [1, E_, D])
                wg = sb(st, "moe_wg", [P, E_])
                before = sb(st, "moe_before", [P, E_ * E_])
                ld = new_loads("moe_loads")
                ld.start(wg[:, :], a["moe_wg"])
                ld.start(before[:, :], a["c_before8"])
                with nc.allow_non_contiguous_dma("one bias per channel"):
                    ld.start(b1[:, :], a["moe_b1"].rearrange("e (f p) -> p (e f)", p=P))
                ld.start(b2[:, :, :], a["moe_b2"].rearrange("(o e) d -> o e d", o=1))
                for e in range(E_):
                    ld.start(w1[:, e, :], a["moe_w1"][e])
                ld.start(w2[:, :, :], a["moe_w2"].rearrange("e (f p) d -> p (e f) d", p=P))
                lg = sb(st, "moe_logits", [P, NT, E_])
                gt = sb(st, "moe_gates", [P, NT, E_])
                cmp_ = sb(st, "moe_cmp", [P, NT, E_ * E_])
                eq = sb(st, "moe_eq", [P, NT, E_ * E_])
                mx = sb(st, "moe_max", [P, NT])
                hbuf = sb(st, "moe_h", [P, 2, FT, BANK])
                acc = sb(st, "moe_acc", [P, NT, D])
                for e in (PE, V, A, G):
                    e.wait(ld.now())
                for b in range(NB):
                    ring = Ring(PE, [(k,) for k in range(8)])
                    done = to_channels(ring, norm, layernorm(hid, norm[:, :, :], b, 1e-6, 3), b)
                    PE.wait(*done)
                    k, (bk,) = ring.take()
                    for i in range(NT):
                        last = nc.tensor.matmul(bank(bk)[:, i * E_:(i + 1) * E_], chans[:, b, PAD + i * P:PAD + (i + 1) * P], wg[:, :],
                                                start=True, stop=True)
                    V.wait(PE.op(last))
                    V.step(nc.vector.tensor_copy(lg[:, :, :], bank(bk)[:, 0:NT * E_].rearrange("p (i e) -> p i e", e=E_)))
                    ring.release(k, V.now())
                    mine = wide(lg[:, :, :].rearrange("p i (e o) -> p i e o", o=1), 3, E_)
                    other = wide(lg[:, :, :].rearrange("p i (o e) -> p i o e", o=1), 2, E_)
                    sq = lambda t: t[:, :, :].rearrange("p i (e o) -> p i e o", o=E_)
                    V.op(nc.vector.tensor_tensor(sq(cmp_), other, mine, ALU.is_gt))
                    V.step(nc.vector.tensor_tensor(sq(eq), other, mine, ALU.is_equal))
                    V.step(nc.vector.tensor_tensor(eq[:, :, :], eq[:, :, :], wide(before[:, :].rearrange("p (o n) -> p o n", o=1), 1, NT), ALU.mult))
                    V.step(nc.vector.tensor_tensor(cmp_[:, :, :], cmp_[:, :, :], eq[:, :, :], ALU.add))
                    V.op(nc.vector.tensor_reduce(gt[:, :, :], sq(cmp_), X, ALU.add))
                    V.step(nc.vector.tensor_reduce(mx[:, :], lg[:, :, :], X, ALU.max))
                    V.step(nc.vector.tensor_scalar(gt[:, :, :], gt[:, :, :], 2.0, None, ALU.is_lt))
                    col = lambda t: wide(t[:, :].rearrange("p (i o) -> p i o", o=1), 2, E_)
                    V.step(nc.vector.tensor_tensor(lg[:, :, :], lg[:, :, :], col(mx), ALU.subtract))
                    A.wait(V.now())
                    p = A.op(nc.scalar.activation(lg[:, :, :], lg[:, :, :], ACT.Exp))
                    V.wait(p)
                    V.step(nc.vector.tensor_tensor(gt[:, :, :], gt[:, :, :], lg[:, :, :], ALU.mult))
                    V.step(nc.vector.tensor_reduce(mx[:, :], gt[:, :, :], X, ALU.add))
                    V.step(nc.vector.reciprocal(mx[:, :], mx[:, :]))
                    V.step(nc.vector.tensor_tensor(gt[:, :, :], gt[:, :, :], col(mx), ALU.mult))
                    V.step(nc.vector.tensor_scalar(gt[:, :, :], gt[:, :, :], mask[:, b, 3:4], None, ALU.mult))
                    barrier()
                    r1 = Ring(PE, [(0,), (1,), (2,), (3,)])
                    r2 = Ring(PE, [(4,), (5,), (6,), (7,)])
                    hread = [None, None]
                    pend = []
                    added = {}

                    def down(item):
                        g, e, s, ready = item
                        PE.wait(ready)
                        k, (bk,) = r2.take()
                        for q in range(4):
                            o = bank(bk)[:, q * D:(q + 1) * D]
                            for f in range(FT):
                                nc.tensor.matmul(o, hbuf[:, s, f, q * P:(q + 1) * P], w2[:, e * FT + f, :], start=(f == 0), stop=False)
                            last = nc.tensor.matmul(o, ones[0:1, :], b2[:, e, :], start=False, stop=True)
                        p = PE.op(last)
                        V.wait(p)
                        for q in range(4):
                            t = 4 * g + q
                            h = hid[:, b * NT + t, :]
                            V.wait(added.get(t))
                            v = added[t] = V.op(nc.vector.scalar_tensor_tensor(h, bank(bk)[:, q * D:(q + 1) * D], gt[:, t, e:e + 1], h, ALU.mult, ALU.add))
                        r2.release(k, v)
                        return p
                    n = 0
                    for g in range(NT // 4):
                        for e in range(E_):
                            s = n % 2
                            n += 1
                            for f in range(FT):
                                k, (bk,) = r1.take()
                                p = PE.op(nc.tensor.matmul(bank(bk), w1[:, e, f * P:(f + 1) * P],
                                                           chans[:, b, PAD + g * BANK:PAD + (g + 1) * BANK], start=True, stop=True))
                                A.wait(p, hread[s])
                                p = A.op(nc.scalar.activation(hbuf[:, s, f, :], bank(bk), ACT.Gelu_apprx_tanh,
                                                              bias=b1[:, e * FT + f:e * FT + f + 1]))
                                r1.release(k, p)
                            pend.append((g, e, s, p))
                            if len(pend) > 1:
                                it = pend.pop(0)
                                hread[it[2]] = down(it)
                    while pend:
                        down(pend.pop(0))
                    barrier()
                    x = res[:, b * NT:(b + 1) * NT, :]
                    V.step(nc.vector.tensor_tensor(x, x, hid[:, b * NT:(b + 1) * NT, :], ALU.add))
                    barrier()

        def phase_E(tag):
            NHE, HDE, NA = 16, 64, 4
            NPAIR = NA // 2
            QC = S // BANK
            with ExitStack() as st:
                def buf(name, shp, dt=F32):
                    return sb(st, "f_" + name + tag, shp, dt)

                wr = buf("wr", [P, NHE])
                br = buf("br", [1, NHE])
                wo = buf("wo", [P, NPAIR, D])
                bo = buf("bo", [P, D])
                before = buf("before", [1, NHE * NHE])
                index = buf("index", [1, NHE])
                ld = new_loads("ffn_loads" + tag)
                ld.start(wr[:, :], a["Wr"])
                ld.start(br[:, :], a["br"].rearrange("(o n) -> o n", o=1))
                ld.start(wo[:, :, :], a["Wo"].rearrange("(j p) d -> p j d", p=P))
                ld.start(bo[:, :], bcast(a["bo"], P))
                ld.start(before[:, :], a["c_before"][0:1, :])
                ld.start(index[:, :], a["c_index"][0:1, :])
                sels = [new_loads(f"ffn_heads{tag}_{b}") for b in range(NB)]
                ws = buf("wqk", [P, NB, 2, NA, 2, HDE])
                wv = buf("wv", [P, NB, NA, HDE])
                bqk = buf("bqk", [P, NB, 2, NA])
                bv = buf("bv", [P, NB, NA, HDE])
                pooled = buf("pooled", [P, 1])
                d = buf("dist", [1, NHE])
                sc = buf("sc", [1, 2])
                rank = buf("rank", [1, NHE])
                pos = buf("pos", [1, NHE])
                idf = buf("idf", [1, NA])
                idi = buf("idi", [1, NB, NA], I32)
                qhh, qmm, qhl, khm, klh = (buf(n, [P, 2, 2, S], BF16) for n in ("qhh", "qmm", "qhl", "khm", "klh"))
                vt = buf("v", [P, 2, NT, 2, HDE])
                pT = buf("pT", [P, 4, NT, P])
                pb = hid[:, :, :].rearrange("p (s i) n -> p s (i n)", s=2)
                cm, eq = (norm[0:1, 2 * n:2 * n + 2, :].rearrange("p a n -> p (a n)").rearrange("p (h o) -> p h o", o=NHE) for n in range(2))
                q32 = norm[:, 0:12, :].rearrange("p (s i) n -> p s (i n)", s=3)
                parts = norm[:, 12:16, :].rearrange("p i n -> p (i n)").bitcast(BF16).rearrange("p (a n) -> p a n", a=2)
                m2 = buf("m2", [P, 4, 2])
                nm = buf("nm", [P, 4])
                rs = buf("rs", [P, 8, 2])
                oT = buf("oT", [P, 2, P])
                for e in (PE, V, A, G, SP):
                    e.wait(ld.now())

                def choose(b):
                    ring = Ring(PE, [(k,) for k in range(8)])
                    done = to_channels(ring, norm, layernorm(res, norm[:, :, :], b, 1e-5), b)
                    V.wait(*done)
                    V.step(nc.vector.tensor_reduce(pooled[:, :], chans[:, b, PAD:PAD + S], X, ALU.add))
                    p = V.step(nc.vector.tensor_scalar(pooled[:, :], pooled[:, :], 1.0 / S, None, ALU.mult))
                    PE.wait(p, *done)
                    k, (bk,) = ring.take()
                    V.wait(PE.op(nc.tensor.matmul(bank(bk)[0:1, 0:NHE], pooled[:, :], wr[:, :], start=True, stop=True)))
                    V.step(nc.vector.tensor_tensor(d[:, :], bank(bk)[0:1, 0:NHE], br[:, :], ALU.add))
                    V.step(nc.vector.tensor_reduce(sc[:, 0:1], d[:, :], X, ALU.max, negate=True))
                    A.wait(V.now())
                    p = A.op(nc.scalar.activation(d[:, :], d[:, :], ACT.Exp, bias=sc[:, 0:1]))
                    V.wait(p)
                    V.step(nc.vector.tensor_reduce(sc[:, 1:2], d[:, :], X, ALU.add))
                    V.step(nc.vector.reciprocal(sc[:, 1:2], sc[:, 1:2]))
                    V.step(nc.vector.tensor_scalar(d[:, :], d[:, :], sc[:, 1:2], None, ALU.mult))
                    mine = wide(d[:, :].rearrange("p (h o) -> p h o", o=1), 2, NHE)
                    other = wide(d[:, :].rearrange("p (o h) -> p o h", o=1), 1, NHE)
                    bf = before[:, :].rearrange("p (h o) -> p h o", o=NHE)
                    V.op(nc.vector.tensor_tensor(cm, other, mine, ALU.is_gt))
                    V.step(nc.vector.tensor_tensor(eq, other, mine, ALU.is_equal))
                    V.step(nc.vector.tensor_tensor(eq, eq, bf, ALU.mult))
                    V.step(nc.vector.tensor_tensor(cm, cm, eq, ALU.add))
                    V.step(nc.vector.tensor_reduce(rank[:, :], cm, X, ALU.add))
                    V.step(nc.vector.tensor_scalar(rank[:, :], rank[:, :], float(NA), None, ALU.is_lt))
                    V.step(nc.vector.tensor_tensor(cm, wide(rank[:, :].rearrange("p (o h) -> p o h", o=1), 1, NHE), bf, ALU.mult))
                    V.step(nc.vector.tensor_reduce(pos[:, :], cm, X, ALU.add))
                    for j in range(NA):
                        V.step(nc.vector.scalar_tensor_tensor(eq[:, j, :], pos[:, :], float(j), rank[:, :], ALU.is_equal, ALU.mult))
                        V.step(nc.vector.tensor_tensor(eq[:, j, :], eq[:, j, :], index[:, :], ALU.mult))
                    V.step(nc.vector.tensor_reduce(idf[:, :], eq[:, 0:NA, :], X, ALU.add))
                    V.step(nc.vector.tensor_copy(idi[:, b, :], idf[:, :]))
                    SP.wait(V.now())
                    sel = sels[b]
                    for j in range(NA):
                        hsel = nc.sync.value_load(idi[0:1, b, j:j + 1], min_val=0, max_val=NHE - 1)
                        at = bass.ds(hsel * HDE, HDE)
                        for n, name in enumerate(("Wq", "Wk")):
                            for r in range(2):
                                sel.start(ws[:, b, n, j, r, :], a[name][:, at])
                        sel.start(wv[:, b, j, :], a["Wv"][:, at])
                        with nc.allow_non_contiguous_dma("one bias per channel"):
                            for n, name in enumerate(("bq", "bk")):
                                for r in range(2):
                                    sel.start(bqk[64 * r:64 * r + 64, b, n, j:j + 1], a[name][at].rearrange("(p o) -> p o", o=1))
                        sel.start(bv[:, b, j, :], wide(a["bv"][at].rearrange("(o n) -> o n", o=1), 0, P))
                    G.wait(V.now())
                    x = res[:, b * NT:(b + 1) * NT, :]
                    pt["bias"] = G.op(nc.gpsimd.tensor_tensor(x, x, wide(bo[:, :].rearrange("p (o n) -> p o n", o=1), 1, NT), ALU.add))

                pt = {}
                for b in range(NB):
                    choose(b)
                PE.wait(V.now(), A.now())

                pairs_ = [(b, jp) for b in range(NB) for jp in range(NPAIR)]
                units = [(n, i, h) for n in range(len(pairs_)) for i in range(NT) for h in range(2)]
                NU = len(units)
                SC = 1.0 / float(np.sqrt(HDE))
                sr = Ring(PE, [(0, 1), (2, 3)])
                tr = Ring(PE, [(4,), (5,)])
                orr = Ring(PE, [(6,)])
                mr = Ring(PE, [(7,)])
                wide_ring = Ring(PE, [(k,) for k in range(8)])

                def piece_front(n, m, c, mr=mr):
                    b, jp = pairs_[n]
                    w = n % 2
                    if m == 0 and jp == 0:
                        for e in (PE, V, A):
                            e.wait(sels[b].now())
                    k, (bk,) = mr.take()
                    if m >= 16:
                        g = m - 16
                        for q in range(4):
                            t = 4 * g + q
                            last = nc.tensor.matmul(bank(bk)[:, q * P:(q + 1) * P], chans[:, b, PAD + t * P:PAD + (t + 1) * P],
                                                    wv[:, b, 2 * jp:2 * jp + 2, :], start=True, stop=True)
                        p = PE.op(last)
                        V.wait(p, pt.get(("av", n - 2)))
                        for q in range(4):
                            p = V.op(nc.vector.tensor_tensor(vt[:, w, 4 * g + q], bank(bk)[:, q * P:(q + 1) * P].rearrange("p (h x) -> p h x", h=2),
                                                             bv[:, b, 2 * jp:2 * jp + 2, :], ALU.add))
                        mr.release(k, p)
                        pt["vready", n] = p
                        return
                    g, h, kq = m // 4, m // 2 % 2, m % 2
                    j, s = 2 * jp + h, c % 3
                    p = PE.op(nc.tensor.matmul(bank(bk), ws[:, b, kq, j, :, :], chans[:, b, PAD + g * BANK:PAD + (g + 1) * BANK],
                                               start=True, stop=True))
                    A.wait(p, pt.get(("piece_read", c - 3)))
                    p = A.op(nc.scalar.activation(q32[:, s, :], bank(bk), ACT.Identity, bias=bqk[:, b, kq, j:j + 1]))
                    mr.release(k, p)
                    V.wait(p, *pt.get(("parts_read", c - 2), ()))
                    hi = qhh[:, w, h, g * BANK:(g + 1) * BANK] if kq == 0 else parts[:, 0, :]
                    p = V.op(nc.vector.tensor_copy(hi, q32[:, s, :]))
                    G.wait(p, G.now())
                    pt["rest", c] = G.op(nc.gpsimd.tensor_tensor(q32[:, s, :], q32[:, s, :], hi, ALU.subtract))
                    pt["hi", c] = p

                def piece_back(n, m, c):
                    if m >= 16:
                        return
                    w = n % 2
                    g, h, kq = m // 4, m // 2 % 2, m % 2
                    s = c % 3
                    cs = slice(g * BANK, (g + 1) * BANK)
                    hi = qhh[:, w, h, cs] if kq == 0 else parts[:, 0, :]
                    mid = qmm[:, w, h, cs] if kq == 0 else parts[:, 1, :]
                    A.wait(pt["rest", c])
                    p = A.op(nc.scalar.copy(mid, q32[:, s, :]))
                    G.wait(p, G.now())
                    V.wait(p)
                    if kq == 0:
                        lo = qhl[64:128, w, h, cs]
                        g1 = G.op(nc.gpsimd.tensor_tensor(lo, q32[64:128, s, :], mid[64:128], ALU.subtract))
                        V.op(nc.vector.tensor_copy(qhl[0:64, w, h, cs], hi[0:64]))
                    else:
                        lo = klh[0:64, w, h, cs]
                        g1 = G.op(nc.gpsimd.tensor_tensor(lo, q32[0:64, s, :], mid[0:64], ALU.subtract))
                        V.op(nc.vector.tensor_copy(khm[0:64, w, h, cs], hi[0:64]))
                        V.op(nc.vector.tensor_copy(khm[64:128, w, h, cs], mid[64:128]))
                        V.op(nc.vector.tensor_copy(klh[64:128, w, h, cs], hi[64:128]))
                    pt["piece_read", c] = g1
                    pt["parts_read", c] = (g1, V.now())
                    pt["qkready", n] = (g1, V.now(), p)

                def scores(u):
                    n, i, h = units[u]
                    w = n % 2
                    qs = slice(i * P, (i + 1) * P)
                    if i == 0 and h == 0:
                        PE.wait(*pt["qkready", n])
                    ks = []
                    for hf in range(2):
                        k, bks = sr.take()
                        for jj in range(2):
                            cs = slice((hf * 2 + jj) * BANK, (hf * 2 + jj + 1) * BANK)
                            nc.tensor.matmul(bank(bks[jj]), qhh[:, w, h, qs], khm[:, w, h, cs], start=True, stop=False)
                            nc.tensor.matmul(bank(bks[jj]), qmm[:, w, h, qs], khm[:, w, h, cs], start=False, stop=False)
                            last = nc.tensor.matmul(bank(bks[jj]), qhl[:, w, h, qs], klh[:, w, h, cs], start=False, stop=True)
                        V.wait(PE.op(last), pt.get(("exp", u - 4)))
                        V.op(nc.vector.tensor_reduce(m2[:, u % 4, hf:hf + 1], psum[:, bks[0]:bks[0] + 2, :].rearrange("p b n -> p (b n)"), X, ALU.max))
                        ks.append((k, bks))
                    V.wait(V.now())
                    pt["max", u] = V.op(nc.vector.tensor_scalar(nm[:, u % 4:u % 4 + 1], m2[:, u % 4, 0:1], m2[:, u % 4, 1:2], -SC, ALU.max, ALU.mult))
                    pt["banks", u] = ks

                def exps(u):
                    A.wait(pt["max", u], pt.get(("turned", u - 2)), pt.get(("rsum", u - 8)))
                    for hf, (k, bks) in enumerate(pt["banks", u]):
                        p = A.op(nc.scalar.activation(pb[:, u % 2, hf * 2 * BANK:(hf + 1) * 2 * BANK],
                                                      psum[:, bks[0]:bks[0] + 2, :].rearrange("p b n -> p (b n)"), ACT.Exp,
                                                      bias=nm[:, u % 4:u % 4 + 1], scale=SC, accum_out=rs[:, u % 8, hf:hf + 1]))
                        sr.release(k, p)
                    pt["exp", u] = p

                def turn(u, g, e):
                    PE.wait(pt["exp", u])
                    k, (bk,) = tr.take()
                    for q in range(4):
                        last = nc.tensor.transpose(bank(bk)[:, q * P:(q + 1) * P], pb[:, u % 2, (4 * g + q) * P:(4 * g + q + 1) * P], ident[:, :])
                    pt["turned", u] = PE.op(last)
                    return k, bk, pt["turned", u]

                def land(u, g, e, t):
                    k, bk, p = t
                    e.wait(p, pt.get(("av_tile", u // 2 - 2)))
                    o = pT[:, u % 4, 4 * g:4 * g + 4, :].rearrange("p q n -> p (q n)")
                    c = A.op(nc.scalar.copy(o, bank(bk))) if e is A else V.op(nc.vector.tensor_copy(o, bank(bk)))
                    tr.release(k, c)
                    pt.setdefault(("pT", u), []).append(c)

                def av(t, half):
                    n, i, _ = units[2 * t]
                    if half == 0:
                        PE.wait(*pt["pT", 2 * t], *pt["pT", 2 * t + 1], pt["vready", n])
                        pt["obank", t] = orr.take()
                    k, (bk,) = pt["obank", t]
                    for kt in range(half * NT // 2, (half + 1) * NT // 2):
                        for h in range(2):
                            last = nc.tensor.matmul(bank(bk)[64 * h:64 * h + 64, 0:P], vt[:, n % 2, kt, h, :], pT[:, (2 * t + h) % 4, kt, :],
                                                    start=(kt == 0), stop=(kt == NT - 1), skip_group_check=True,
                                                    tile_position=(0, 64 * h))
                    if half == 1:
                        pt["av_tile", t] = pt["av", n] = p = PE.op(last)
                        V.wait(p, pt.get(("proj", t - 2)))
                        c = V.op(nc.vector.tensor_copy(oT[:, t % 2, :], bank(bk)[:, 0:P]))
                        orr.release(k, c)
                        pt["oT", t] = c
                        r = rs[:, (2 * t) % 8:(2 * t) % 8 + 2, :]
                        V.wait(pt["exp", 2 * t + 1])
                        V.step(nc.vector.tensor_tensor(r[:, :, 0], r[:, :, 0], r[:, :, 1], ALU.add))
                        pt["recip", t] = V.op(nc.vector.reciprocal(r[:, :, 0], r[:, :, 0]))

                def project(t):
                    n, i, _ = units[2 * t]
                    b, jp = pairs_[n]
                    PE.wait(pt["oT", t])
                    k, (bk,) = mr.take()
                    for h in range(2):
                        PE.wait(PE.now() if h else None)
                        pt["proj", t] = PE.op(nc.tensor.matmul(bank(bk)[:, h * D:(h + 1) * D], oT[64 * h:64 * h + 64, t % 2, :],
                                                               wo[64 * h:64 * h + 64, jp, :], start=True, stop=True))
                    x = res[:, b * NT + i, :]
                    V.wait(pt["proj", t], pt["recip", t], pt["bias"])
                    for h in range(2):
                        p = V.step(nc.vector.scalar_tensor_tensor(x, bank(bk)[:, h * D:(h + 1) * D], rs[:, (2 * t + h) % 8, 0:1], x, ALU.mult, ALU.add))
                    mr.release(k, p)
                    pt["rsum", 2 * t] = pt["rsum", 2 * t + 1] = p

                NPIECE = 20
                for m in range(NPIECE):
                    piece_front(0, m, m, wide_ring)
                    if m:
                        piece_back(0, m - 1, m - 1)
                PE.wait(V.now(), A.now())
                scores(0)
                exps(0)
                for u in range(NU + 3):
                    if u + 1 < NU:
                        scores(u + 1)
                    ts = {}
                    if u < NU:
                        ts[0] = turn(u, 0, A)
                        land(u, 0, A, ts[0])
                        ts[1] = turn(u, 1, A)
                        land(u, 1, A, ts[1])
                    t, half = (u - 2) // 2, (u - 2) % 2
                    if u >= 2 and 2 * t < NU:
                        av(t, half)
                    if u < NU:
                        for g in (2, 3):
                            land(u, g, V, turn(u, g, V))
                    if u + 1 < NU:
                        exps(u + 1)
                    if u >= 4 and u % 2 == 0:
                        project((u - 4) // 2)
                    if u < NU:
                        n, i, h = units[u]
                        m = 2 * i + h
                        c = NPIECE * (n + 1) + m
                        if n + 1 < len(pairs_):
                            if m < NPIECE:
                                piece_front(n + 1, m, c)
                            if 1 <= m <= NPIECE:
                                piece_back(n + 1, m - 1, c - 1)
                barrier()

        def phase_F():
            HID = a["W_q"].shape[1]
            with ExitStack() as st:
                w = sb(st, "d_w", [P, 3 * HID])
                bias = sb(st, "d_b", [P, 3, HID])
                wo = sb(st, "d_wo", [P, HID])
                bo = sb(st, "d_bo", [P, HID])
                ld = new_loads("diag_loads")
                for n, name in enumerate(("q", "k", "v")):
                    ld.start(w[:, n * HID:(n + 1) * HID], a["W_" + name])
                    ld.start(bias[:, n, :], bcast(a["b_" + name], P))
                ld.start(wo[:, :], a["W_o"])
                ld.start(bo[:, :], bcast(a["b_o"], P))
                qf = sb(st, "d_qk", [P, 2, 2 * HID])
                vf = sb(st, "d_v", [P, 2, HID])
                rest = sb(st, "d_rest", [P, 2 * HID])
                part = sb(st, "d_parts", [P, 3, 2 * HID], BF16)
                uq = sb(st, "d_q_rows", [P, 2, NH, ROWS], BF16)
                uk = sb(st, "d_k_rows", [P, 2, NH, ROWS], BF16)
                qT = sb(st, "d_qT", [ROWS, 2, NH * P], BF16)
                kT = sb(st, "d_kT", [ROWS, 2, NH * P], BF16)
                dg = sb(st, "d_diag", [P, 3, NH])
                dj = sb(st, "d_diag_terms", [P, HID])
                mh = sb(st, "d_negmax", [P, 2, NH, 2])
                sh = sb(st, "d_sums", [P, 2, NH, 2])
                mm = sb(st, "d_negmax_all", [P, NH])
                cf = sb(st, "d_coeff", [P, NH, 2])
                junk = sb(st, "d_junk", [P, 3, 2 * BANK], BF16)
                junked = []
                ov = sb(st, "d_out", [P, HID])
                oT = sb(st, "d_oT", [P, HID])
                for e in (PE, V, A, G):
                    e.wait(ld.now())
                G.op(nc.gpsimd.memset(uq[:, :, :, NG * HD:ROWS], 0.0))
                G.op(nc.gpsimd.memset(uk[:, :, :, NG * HD:ROWS], 0.0))
                SCALE = float(1.0 / np.sqrt(np.float32(HID)))
                V.op(nc.vector.tensor_scalar(w[:, 0:2 * HID], w[:, 0:2 * HID], SCALE, None, ALU.mult))
                V.op(nc.vector.tensor_scalar(bias[:, 0:2, :], bias[:, 0:2, :], SCALE, None, ALU.mult))
                for b in range(NB):
                    ring = Ring(PE, [(k,) for k in range(8)])
                    done = to_channels(ring, norm, layernorm(res, norm[:, :, :], b, 1e-5), b)
                    V.wait(*done)
                barrier()
                V.op(nc.vector.tensor_tensor(res[:, :, :], res[:, :, :], wide(bo[:, :].rearrange("p (o n) -> p o n", o=1), 1, R), ALU.add))
                tr = Ring(PE, [(0,), (1,)])
                sr = Ring(PE, [(2, 3), (4, 5), (6, 7)])
                pt = {}

                def prep(T):
                    b, i, s = T // NT, T % NT, T % 2
                    k, (bk,) = tr.take()
                    p = PE.op(nc.tensor.matmul(bank(bk)[:, 0:3 * HID], chans[:, b, PAD + i * P:PAD + (i + 1) * P], w[:, :], start=True, stop=True))
                    yield
                    V.wait(p, pt.get(("rest", T - 1)), pt.get(("terms", T - 1)), pt.get(("closed", T - 2)))
                    V.op(nc.vector.tensor_tensor(qf[:, s, :], bank(bk)[:, 0:2 * HID], bias[:, 0:2, :].rearrange("p n h -> p (n h)"), ALU.add))
                    p = V.op(nc.vector.tensor_tensor(vf[:, s, :], bank(bk)[:, 2 * HID:3 * HID], bias[:, 2, :], ALU.add))
                    tr.release(k, p)
                    V.wait(p, pt.get(("spread", T - 1)))
                    hi = V.op(nc.vector.tensor_copy(part[:, 0, :], qf[:, s, :]))
                    G.wait(p, pt.get(("diag", T - 1)), G.now())
                    pt["terms", T] = G.op(nc.gpsimd.tensor_tensor(dj[:, :], qf[:, s, 0:HID], qf[:, s, HID:2 * HID], ALU.mult))
                    G.wait(hi, G.now())
                    r = G.op(nc.gpsimd.tensor_tensor(rest[:, :], qf[:, s, :], part[:, 0, :], ALU.subtract))
                    yield
                    yield
                    V.wait(r, pt.get(("closed", T - 3)))
                    mid = V.op(nc.vector.tensor_copy(part[:, 1, :], rest[:, :]))
                    pt["diag", T] = V.op(nc.vector.tensor_reduce(dg[:, T % 3, :], dj[:, :].rearrange("p (h x) -> p h x", x=HD), X, ALU.add))
                    G.wait(mid, G.now())
                    lo = G.op(nc.gpsimd.tensor_tensor(part[:, 2, :], rest[:, :], part[:, 1, :], ALU.subtract))
                    pt["rest", T] = lo
                    yield
                    yield
                    V.wait(lo, pt.get(("turned", T - 2)))
                    G.wait(pt.get(("turned", T - 2)))
                    qr = uq[:, s, :, 0:NG * HD].rearrange("p h (i j x) -> p h i j x", i=3, j=3)
                    kr = uk[:, s, :, 0:NG * HD].rearrange("p h (i j x) -> p h i j x", i=3, j=3)
                    for g in range(3):
                        for c in range(3):
                            V.op(nc.vector.tensor_copy(qr[:, :, g, c, :], part[:, g, 0:HID].rearrange("p (h x) -> p h x", x=HD)))
                        for c in range(3):
                            G.wait(G.now())
                            G.op(nc.gpsimd.tensor_copy(kr[:, :, c, g, :], part[:, g, HID:2 * HID].rearrange("p (h x) -> p h x", x=HD)))
                        yield
                    pt["spread", T] = G.now()
                    spread_q = V.now()
                    yield
                    PE.wait(spread_q)
                    for u, dst in ((uq, qT), (uk, kT)):
                        for g in range(2):
                            if u is uk and g == 0:
                                PE.wait(pt["spread", T])
                            k, (bk,) = tr.take()
                            bvw = psum[0:ROWS, bk, :].bitcast(BF16)
                            for q in range(8):
                                p = nc.tensor.transpose(bvw[:, q * P:(q + 1) * P], u[:, s, 8 * g + q, :], identb[:, :])
                                if q == 7:
                                    p = PE.op(p)
                                if q % 4 == 3:
                                    yield
                            A.wait(p, pt.get(("scored", T - 2)))
                            c = A.op(nc.scalar.copy(dst[:, s, g * 8 * P:(g + 1) * 8 * P], bvw))
                            tr.release(k, c)
                    pt["turned", T] = p
                    pt["rows", T] = c

                def score(T, jb, hf):
                    s = T % 2
                    k, bks = sr.take()
                    for jj in range(2):
                        c = hf * 2 + jj
                        last = nc.tensor.matmul(bank(bks[jj]), kT[:, s, jb * P:(jb + 1) * P], qT[:, s, c * BANK:(c + 1) * BANK], start=True, stop=True)
                    blk = psum[:, bks[0]:bks[0] + 2, :].rearrange("p b n -> p (b n)")
                    pt["scored", T] = PE.op(last)
                    V.wait(pt["scored", T])
                    p = V.op(nc.vector.tensor_reduce(mh[:, s, jb, hf:hf + 1], blk, X, ALU.max, negate=True))
                    A.wait(p, junked[-3] if len(junked) > 2 else None)
                    p = A.op(nc.scalar.activation(junk[:, len(junked) % 3, :], blk, ACT.Exp, bias=mh[:, s, jb, hf:hf + 1],
                                                  accum_out=sh[:, s, jb, hf:hf + 1]))
                    junked.append(p)
                    sr.release(k, p)
                    pt["summed", T] = p

                def close(T):
                    s = T % 2
                    V.wait(pt["summed", T])
                    V.step(nc.vector.tensor_tensor(mm[:, :], mh[:, s, :, 0], mh[:, s, :, 1], ALU.min))
                    for hf in range(2):
                        V.op(nc.vector.tensor_tensor(cf[:, :, hf], mm[:, :], mh[:, s, :, hf], ALU.subtract))
                    d3 = dg[:, T % 3, :]
                    p = V.op(nc.vector.tensor_tensor(d3, d3, mm[:, :], ALU.add))
                    yield
                    A.wait(p)
                    A.op(nc.scalar.activation(cf[:, :, :], cf[:, :, :], ACT.Exp))
                    p = A.op(nc.scalar.activation(d3, d3, ACT.Exp))
                    yield
                    V.wait(p)
                    V.step(nc.vector.tensor_tensor(cf[:, :, :], cf[:, :, :], sh[:, s, :, :], ALU.mult))
                    V.step(nc.vector.tensor_tensor(mm[:, :], cf[:, :, 0], cf[:, :, 1], ALU.add))
                    V.step(nc.vector.reciprocal(mm[:, :], mm[:, :]))
                    V.step(nc.vector.tensor_tensor(mm[:, :], mm[:, :], d3, ALU.mult))
                    p = V.op(nc.vector.tensor_tensor(ov[:, :].rearrange("p (h x) -> p h x", x=HD), vf[:, s, :].rearrange("p (h x) -> p h x", x=HD),
                                                     wide(mm[:, :].rearrange("p (h o) -> p h o", o=1), 2, HD), ALU.mult))
                    pt["closed", T] = p
                    yield
                    yield
                    PE.wait(p)
                    k, (bk,) = tr.take()
                    p = PE.op(nc.tensor.transpose(bank(bk)[:, 0:P], ov[:, :], ident[:, :]))
                    yield
                    V.wait(p)
                    c = V.op(nc.vector.tensor_copy(oT[:, :], bank(bk)[:, 0:P]))
                    tr.release(k, c)
                    yield
                    yield
                    PE.wait(c)
                    k, (bk,) = tr.take()
                    p = PE.op(nc.tensor.matmul(bank(bk)[:, 0:D], oT[:, :], wo[:, :], start=True, stop=True))
                    yield
                    V.wait(p)
                    x = res[:, T, :]
                    c = V.op(nc.vector.tensor_tensor(x, x, bank(bk)[:, 0:D], ALU.add))
                    tr.release(k, c)

                for _ in prep(0):
                    pass
                for T in range(R):
                    PE.wait(pt["rows", T])
                    side = []
                    if T >= 1:
                        side.append(close(T - 1))
                    if T + 1 < R:
                        side.append(prep(T + 1))
                    for jb in range(NH):
                        for hf in range(2):
                            score(T, jb, hf)
                            if side and next(side[0], "end") == "end":
                                side.pop(0)
                    for g in side:
                        for _ in g:
                            pass
                for _ in close(R - 1):
                    pass
                barrier()

        run = {"H": phase_H, "M": phase_M, "T": phase_T, "C": phase_C, "D": phase_D,
               "E": lambda: phase_E("_1"), "F": phase_F, "E2": lambda: phase_E("_2")}
        for ph in phases:
            run[ph]()
        store = new_loads("store")
        barrier()
        store.start(out.rearrange("b (i p) d -> p (b i) d", p=P), res[:, :, :])
        SP.wait(store.now())


def kernel(**inputs):
    import concourse.bacc as bacc
    from concourse.bass_utils import run_bass_kernel_spmd

    nc = bacc.Bacc("TRN2", target_bir_lowering=False, num_devices=1)
    arrays, aps = {}, {}
    for name, value in {**inputs, **constants()}.items():
        short = name.replace("L0_attn_a_", "").replace("L0_attn_b_", "").replace("L0_ffn_", "")
        v = np.ascontiguousarray(value)
        if v.ndim == 0:
            v = v.reshape(1)
        arrays["in_" + short] = v
        aps[short] = nc.dram_tensor("in_" + short, v.shape, mybir.dt.from_np(v.dtype), kind="ExternalInput").ap()
    shape = inputs["L0_attn_a_hidden_states"].shape
    out = nc.dram_tensor("out", shape, F32, kind="ExternalOutput").ap()
    build(nc, aps, out, shape)
    r = run_bass_kernel_spmd(nc, [arrays], core_ids=[0])
    return r.results[0]["out"]
```

```python
from contextlib import ExitStack

import numpy as np
import concourse.bass as bass
from concourse import mybir
from concourse.alu_op_type import AluOpType as ALU

F32, BF16, I32 = mybir.dt.float32, mybir.dt.bfloat16, mybir.dt.int32
ACT = mybir.ActivationFunctionType
X = mybir.AxisListType.X

P = 128
D = 128
BANK = 512
NEG_LOG = 7


class Engine:

    def __init__(self, queue, sem):
        self.q, self.sem, self.count, self.seen = queue, sem, 0, {}

    def op(self, ins):
        ins.then_inc(self.sem, 1)
        self.count += 1
        return (self.sem, self.count)

    def step(self, ins):
        point = self.op(ins)
        self.wait(point)
        return point

    def now(self):
        return (self.sem, self.count)

    def wait(self, *points):
        for p in points:
            if p is None or p[1] <= 0 or self.seen.get(p[0].name, 0) >= p[1]:
                continue
            self.q.wait_ge(p[0], p[1])
            self.seen[p[0].name] = p[1]


class Loads:

    def __init__(self, engine, sem):
        self.e, self.sem, self.count = engine, sem, 0

    def start(self, dst, src):
        self.e.q.dma_start(dst, src).then_inc(self.sem, 16)
        self.count += 16
        return (self.sem, self.count)

    def now(self):
        return (self.sem, self.count)


class Ring:

    def __init__(self, pe, groups):
        self.pe, self.groups, self.free, self.at = pe, groups, [None] * len(groups), 0

    def take(self):
        k = self.at
        self.at = (k + 1) % len(self.groups)
        self.pe.wait(self.free[k])
        return k, self.groups[k]

    def release(self, k, point):
        self.free[k] = point


def wide(ap, dim, n):
    shape = list(ap.shape)
    shape[dim] = n
    return ap.broadcast_to(shape)


def level_masks():
    s, t = np.arange(P)[:, None], np.arange(P)[None, :]
    sums, pairs = np.zeros((P, 9, P), np.float32), np.zeros((P, NEG_LOG, P), np.float32)
    for l in range(NEG_LOG):
        h = 1 << l
        same = (s // (2 * h)) == (t // (2 * h))
        s2, t2 = (s % (2 * h)) >= h, (t % (2 * h)) >= h
        sums[:, l] = same & ((~t2 & ~s2 & (s > t)) | (t2 & s2 & (s <= t)))
        pairs[:, l] = same & ~s2 & t2
    sums[:, 7] = s > t
    sums[:, 8] = s <= t
    return sums, pairs


def constants():
    sums, pairs = level_masks()
    h, o = np.arange(16)[:, None], np.arange(16)[None, :]
    before = (o < h).astype(np.float32).reshape(1, 256)
    return {
        "c_ident": np.eye(P, dtype=np.float32),
        "c_sums": sums,
        "c_pairs": pairs,
        "c_before": np.repeat(before, P, 0),
        "c_index": np.repeat(np.arange(16, dtype=np.float32)[None], P, 0),
        "c_before8": np.repeat((np.arange(8)[None] < np.arange(8)[:, None]).astype(np.float32).reshape(1, 64), P, 0),
    }


def build(nc, a, out, shape, phases=("H", "M", "T", "C", "D", "E", "F", "E2")):
    NB, S, _ = shape
    NT = S // P
    R = NB * NT
    ctx = ExitStack()
    with ctx:
        sem = lambda n: ctx.enter_context(nc.semaphore(n))
        PE, V, A, G = (Engine(q, sem(n)) for q, n in
                       ((nc.tensor, "pe_done"), (nc.vector, "dve_done"), (nc.scalar, "act_done"),
                        (nc.gpsimd, "pool_done")))
        SP = Engine(nc.sync, sem("sp_done"))
        engines = (PE, V, A, G, SP)
        loads = []

        def new_loads(name, engine=None):
            l = Loads(engine or SP, sem(name))
            loads.append(l)
            return l

        def barrier():
            points = [e.now() for e in engines] + [l.now() for l in loads]
            for e in engines:
                e.wait(*points)

        def sb(stack, name, shp, dt=F32):
            return stack.enter_context(nc.sbuf_tensor(name, shp, dt))

        psum = ctx.enter_context(nc.psum_tensor("psum", [P, 8, BANK], F32))
        bank = lambda k: psum[:, k, :]

        def bcast(ap, n):
            return wide(ap.rearrange("(o n) -> o n", o=1), 0, n)

        res = sb(ctx, "residual", [P, R, D])
        hid = sb(ctx, "hidden", [P, R, D])
        norm = sb(ctx, "normed", [P, NT, D])
        PAD = 4
        chans = sb(ctx, "normed_channels", [P, NB, PAD + S])
        ident = sb(ctx, "ident", [P, P])
        identb = sb(ctx, "ident_bf16", [P, P], BF16)
        stats = sb(ctx, "ln_stats", [P, NT, 6])
        mv = sb(ctx, "ln_mean_var", [P, NT, 2])
        rstd = sb(ctx, "ln_rstd", [P, NT])
        ones = sb(ctx, "ones", [P, P])
        mask = sb(ctx, "block_masks", [P, NB, 4])
        ln_g = sb(ctx, "ln_gains", [P, 4, D])
        ln_b = sb(ctx, "ln_biases", [P, 4, D])

        first = new_loads("first_loads")
        xt = a["hidden_states"].rearrange("b (i p) d -> p (b i) d", p=P)
        first.start(ident[:, :], a["c_ident"])
        for b in range(NB):
            first.start(res[:, b * NT:(b + 1) * NT, :], xt[:, b * NT:(b + 1) * NT, :])
        for j in range(4):
            first.start(ln_g[:, j, :], bcast(a["ln_g"][j, :], P))
            first.start(ln_b[:, j, :], bcast(a["ln_b"][j, :], P))
        for e in (PE, V, A, G):
            e.wait(first.now())
        V.op(nc.vector.memset(ones[:, :], 1.0))
        V.op(nc.vector.memset(chans[:, :, 0:PAD], 0.0))
        V.step(nc.vector.tensor_copy(identb[:, :], ident[:, :]))

        def layernorm_steps(src, dst, b, eps, j=None):
            t0 = b * NT
            for i in range(NT):
                V.op(nc.vector.bn_stats(stats[:, i, :], src[:, t0 + i, :]))
                if i % 4 == 3:
                    yield
            V.wait(V.now())
            for i in range(NT):
                V.op(nc.vector.bn_aggr(mv[:, i, :], stats[:, i, :]))
            V.wait(V.now())
            var = V.op(nc.vector.tensor_scalar(rstd[:, :], mv[:, :, 1], eps, None, ALU.add))
            A.wait(var)
            std = A.op(nc.scalar.activation(rstd[:, :], rstd[:, :], ACT.Sqrt))
            yield
            V.wait(std)
            V.step(nc.vector.reciprocal(rstd[:, :], rstd[:, :]))
            yield
            for i in range(NT):
                V.op(nc.vector.tensor_scalar(dst[:, i, :], src[:, t0 + i, :], mv[:, i, 0:1],
                                             rstd[:, i:i + 1], ALU.subtract, ALU.mult))
                if i % 4 == 3:
                    yield
            if j is not None:
                V.wait(V.now())
                V.step(nc.vector.tensor_tensor(dst, dst, wide(ln_g[:, j:j + 1, :], 1, NT), ALU.mult))
                yield
                V.step(nc.vector.tensor_tensor(dst, dst, wide(ln_b[:, j:j + 1, :], 1, NT), ALU.add))
                yield

        def layernorm(src, dst, b, eps, j=None):
            for _ in layernorm_steps(src, dst, b, eps, j):
                pass
            return V.now()

        def to_channels_steps(ring, src, ready, b, n=NT, dst=None, off=PAD):
            dst = chans[:, b, :] if dst is None else dst[:, :]
            PE.wait(ready)
            for g in range(n // 4):
                k, (bk,) = ring.take()
                for q in range(4):
                    last = nc.tensor.transpose(bank(bk)[:, q * P:(q + 1) * P], src[:, 4 * g + q, :], ident[:, :])
                done = PE.op(last)
                e = A if g % 2 else V
                e.wait(done)
                o = dst[:, off + BANK * g:off + BANK * (g + 1)]
                ring.release(k, A.op(nc.scalar.copy(o, bank(bk))) if g % 2 else
                             V.op(nc.vector.tensor_copy(o, bank(bk))))
                yield

        def to_channels(*args, **kw):
            for _ in to_channels_steps(*args, **kw):
                pass
            return (A.now(), V.now())

        def phase_H():
            with ExitStack() as st:
                pooled = sb(st, "pooled", [P, NB])
                pooled_all = sb(st, "pooled_all", [P, NB, P])
                router_w = sb(st, "router_w", [P, 4])
                router_b = sb(st, "router_b", [P, 4])
                z = sb(st, "router_z", [P, NB, 4])
                ld = new_loads("router_loads")
                ld.start(router_w[:, :], a["router_w"])
                ld.start(router_b[:, :], bcast(a["router_b"], P))
                ring = Ring(PE, [(k,) for k in range(8)])
                for b in range(NB):
                    ready = layernorm(res, hid[:, b * NT:(b + 1) * NT, :], b, 1e-5)
                    PE.wait(ready)
                    k, (bk,) = ring.take()
                    for i in range(NT):
                        last = nc.tensor.matmul(bank(bk)[:, 0:1], hid[:, b * NT + i, :], ones[:, 0:1],
                                                start=(i == 0), stop=(i == NT - 1))
                    V.wait(PE.op(last))
                    V.step(nc.vector.tensor_scalar(pooled[:, b:b + 1], bank(bk)[:, 0:1], 1.0 / S, None, ALU.mult))
                    pool = V.op(nc.vector.tensor_scalar(pooled_all[:, b, :], ones[:, :], pooled[:, b:b + 1], None, ALU.mult))
                    ring.release(k, V.now())
                    PE.wait(pool, ld.now())
                    k, (bk,) = ring.take()
                    done = PE.op(nc.tensor.matmul(bank(bk)[:, 0:4], pooled_all[:, b, :], router_w[:, :],
                                                  start=True, stop=True))
                    V.wait(done, ld.now())
                    s = V.op(nc.vector.tensor_tensor(z[:, b, :], bank(bk)[:, 0:4], router_b[:, :], ALU.add))
                    ring.release(k, s)
                    A.wait(s)
                    e = A.op(nc.scalar.activation(z[:, b, :], z[:, b, :], ACT.Exp, scale=-1.0))
                    V.wait(e)
                    V.step(nc.vector.tensor_scalar(z[:, b, :], z[:, b, :], 1.0, None, ALU.add))
                    V.step(nc.vector.reciprocal(z[:, b, :], z[:, b, :]))
                    V.step(nc.vector.tensor_scalar(mask[:, b, :], z[:, b, :], 0.3, None, ALU.is_gt))
                barrier()

        def phase_M():
            DI = a["m_conv"].shape[1]
            N = a["m_wbc"].shape[1] // 2
            C2 = DI // P
            CK = a["m_conv"].shape[0]
            with ExitStack() as st:
                win = sb(st, "m_win", [P, 2 * DI])
                taps = sb(st, "m_taps", [P, CK, DI])
                wbc = sb(st, "m_wbc", [P, C2, 2 * N])
                wout = sb(st, "m_wout", [P, C2, D])
                neg_a = sb(st, "m_neg_a", [P, DI])
                wdt = sb(st, "m_wdt", [P, DI])
                dtb = sb(st, "m_dtb", [P, DI])
                dskip = sb(st, "m_dskip", [P, DI])
                sums = sb(st, "level_sums", [P, 9, P])
                pairs = sb(st, "level_pairs", [P, NEG_LOG, P])
                ld = new_loads("mamba_loads")
                ld.start(win[:, :], a["m_win"])
                for c in range(CK):
                    ld.start(taps[:, c, :], bcast(a["m_conv"][c, :], P))
                ld.start(wbc[:, :, :], a["m_wbc"].rearrange("(k p) n -> p k n", p=P))
                ld.start(wout[:, :, :], a["m_wout"].rearrange("(k p) n -> p k n", p=P))
                for t, n in ((neg_a, "m_alog"), (wdt, "m_wdt"), (dtb, "m_dtb"), (dskip, "m_dskip")):
                    ld.start(t[:, :], bcast(a[n], P))
                ld.start(sums[:, :, :], a["c_sums"])
                ld.start(pairs[:, :, :], a["c_pairs"])
                V.wait(ld.now()); A.wait(ld.now()); G.wait(ld.now()); PE.wait(ld.now())
                for c in range(CK):
                    V.op(nc.vector.tensor_tensor(taps[:, c, :], taps[:, c, :], win[:, 0:DI], ALU.mult))
                taps_ready = V.now()
                neg = A.op(nc.scalar.activation(neg_a[:, :], neg_a[:, :], ACT.Exp))
                V.wait(neg)
                V.step(nc.vector.tensor_scalar(neg_a[:, :], neg_a[:, :], -1.0, None, ALU.mult))
                G.wait(V.now())

                xz = sb(st, "m_xz", [P, NT, 2 * DI])
                dta = sb(st, "m_dta", [P, NT, DI])
                dtx = sb(st, "m_dtx", [P, NT, DI])
                Q4 = 4
                xT = sb(st, "m_xT", [P, 2, C2, P])
                bctok = sb(st, "m_bc", [P, 3, 2 * N])
                bct = sb(st, "m_bcT", [N, 3, 2, P])
                gtt = sb(st, "m_gdiag", [P, 3, 1])
                gjunk = sb(st, "m_gjunk", [P, N])
                gm = sb(st, "m_pairs", [P, 3, NEG_LOG, P])
                dec = sb(st, "m_decay", [P, 2, 9, DI])
                total = sb(st, "m_total", [N, 2, DI])
                val = sb(st, "m_val", [P, 2, 8, DI])
                skip = sb(st, "m_skip", [P, 2, DI])
                zz = norm[:, :, :].rearrange("p (l c) n -> p l (c n)", l=8)
                yy = sb(st, "m_y", [P, DI])
                yT = sb(st, "m_yT", [P, C2, P])
                state = sb(st, "m_state", [N, DI])

                for b in range(NB):
                    ring = Ring(PE, [(k,) for k in range(8)])
                    if b == 0:
                        done = to_channels(ring, norm, layernorm(hid, norm[:, :, :], b, 1e-6, 0), b)
                        V.wait(PE.now())
                        beside = layernorm_steps(hid, norm[:, :, :], 1, 1e-6, 0)
                    PE.wait(*done, taps_ready)
                    row = lambda t: wide(t[:, :].rearrange("p (o n) -> p o n", o=1), 1, Q4)
                    groups = [slice(Q4 * q, Q4 * (q + 1)) for q in range(NT // Q4)]
                    vp, ep, wp, cp, lp, scaled = [], [], [], [], [], []
                    silu = []
                    for i in range(NT):
                        k, (bk,) = ring.take()
                        t0 = PAD + i * P
                        for c in range(CK):
                            nc.tensor.matmul(bank(bk)[:, 0:DI], chans[:, b, t0 + c - CK + 1:t0 + c - CK + 1 + P],
                                             taps[:, c, :], start=(c == 0), stop=(c == CK - 1))
                        p = PE.op(nc.tensor.matmul(bank(bk)[:, DI:2 * DI], chans[:, b, t0:t0 + P], win[:, DI:2 * DI],
                                                   start=True, stop=True))
                        A.wait(p)
                        silu.append(A.op(nc.scalar.activation(xz[:, i, :], bank(bk), ACT.Silu)))
                        ring.release(k, silu[-1])
                        q, g = i // Q4, groups[i // Q4]
                        if i % Q4 == Q4 - 1:
                            V.wait(silu[-1])
                            V.step(nc.vector.tensor_tensor(dtx[:, g, :], xz[:, g, 0:DI], row(wdt), ALU.mult))
                            vp.append(V.op(nc.vector.tensor_tensor(dtx[:, g, :], dtx[:, g, :], row(dtb), ALU.add)))
                        if i == 5 and b == 0:
                            for _ in beside:
                                pass
                            normed = V.now()
                    if b == 0:
                        done = to_channels(ring, norm, normed, 1)
                    wbuf = val[:, :, :, :].rearrange("p a l n -> p (a l) n")
                    for q, g in enumerate(groups[len(ep):], len(ep)):
                        A.wait(vp[q])
                        ep.append(A.op(nc.scalar.activation(dta[:, g, :], dtx[:, g, :], ACT.Abs)))
                    for q, g in enumerate(groups):
                        A.wait(ep[q])
                        ep[q] = A.op(nc.scalar.activation(dta[:, g, :], dta[:, g, :], ACT.Exp, scale=-1.0))
                    for q, g in enumerate(groups):
                        V.wait(ep[q])
                        wp.append(V.op(nc.vector.tensor_scalar(wbuf[:, g, :], dta[:, g, :], 1.0, None, ALU.add)))
                    for q, g in enumerate(groups):
                        V.wait(wp[q])
                        cp.append(V.op(nc.vector.scalar_tensor_tensor(dta[:, g, :], wbuf[:, g, :], 1.0, dta[:, g, :], ALU.subtract, ALU.subtract)))
                    for q, g in enumerate(groups):
                        A.wait(cp[q])
                        lp.append(A.op(nc.scalar.activation(wbuf[:, g, :], wbuf[:, g, :], ACT.Ln)))
                    for q, g in enumerate(groups):
                        V.wait(lp[q])
                        V.step(nc.vector.tensor_tensor(wbuf[:, g, :], wbuf[:, g, :], dta[:, g, :], ALU.subtract))
                        p = V.op(nc.vector.scalar_tensor_tensor(wbuf[:, g, :], dtx[:, g, :], 0.0, wbuf[:, g, :], ALU.max, ALU.add))
                        G.wait(p)
                        scaled.append(G.op(nc.gpsimd.tensor_tensor(dta[:, g, :], wbuf[:, g, :], row(neg_a), ALU.mult)))
                        V.wait(p)
                        V.op(nc.vector.tensor_tensor(dtx[:, g, :], wbuf[:, g, :], xz[:, g, 0:DI], ALU.mult))
                    V.step(nc.vector.memset(state[:, :], 0.0))
                    PE.wait(A.now(), V.now())
                    G.wait(V.now(), A.now(), G.now())

                    misc = Ring(PE, [(0,), (1,)])
                    dring = Ring(PE, [(2,), (3,)])
                    yfree = [None]
                    pt = {}

                    def chunk_front(i, j):
                        s = i % 2
                        PE.wait(scaled[i // Q4])
                        kd, (bd,) = dring.take()
                        for h in range(2):
                            if 2 * j + h < 9:
                                last = nc.tensor.matmul(bank(bd)[:, h * DI:(h + 1) * DI], sums[:, 2 * j + h, :], dta[:, i, :],
                                                        start=True, stop=True)
                            else:
                                last = nc.tensor.matmul(bank(bd)[0:N, h * DI:(h + 1) * DI], ones[:, 0:N], dta[:, i, :],
                                                        start=True, stop=True)
                        A.wait(PE.op(last), pt.get(("z_read", i - 2)), pt.get(("state", i - 2)))
                        if j < 4:
                            p = A.op(nc.scalar.activation(dec[:, s, 2 * j:2 * j + 2, :],
                                                          bank(bd).rearrange("p (l n) -> p l n", l=2), ACT.Exp))
                            G.wait(p, pt.get(("pe_back", i - 2)))
                            pt["val", i] = G.op(nc.gpsimd.tensor_tensor(val[:, s, 2 * j:2 * j + 2, :], dec[:, s, 2 * j:2 * j + 2, :],
                                                                        wide(dtx[:, i:i + 1, :], 1, 2), ALU.mult))
                        else:
                            A.op(nc.scalar.activation(dec[:, s, 8, :], bank(bd)[:, 0:DI], ACT.Exp))
                            p = A.op(nc.scalar.activation(total[:, s, :], bank(bd)[0:N, DI:2 * DI], ACT.Exp))
                            pt["decays", i] = p
                            G.wait(pt.get(("y_read", i - 2)))
                            pt["skip", i] = G.op(nc.gpsimd.tensor_tensor(skip[:, s, :], xz[:, i, 0:DI], dskip[:, :], ALU.mult))
                        dring.release(kd, p)

                    def chunk_turn(i):
                        k, (bk,) = misc.take()
                        for c in range(C2):
                            last = nc.tensor.transpose(bank(bk)[:, c * P:(c + 1) * P], xz[:, i, c * P:(c + 1) * P], ident[:, :])
                        A.wait(PE.op(last), pt.get(("bc_made", i - 2)))
                        pt["xT", i] = A.op(nc.scalar.copy(xT[:, i % 2], bank(bk)[:, 0:C2 * P].rearrange("p (c t) -> p c t", c=C2)))
                        misc.release(k, pt["xT", i])

                    def chunk_bc(i):
                        s = i % 3
                        PE.wait(pt["xT", i])
                        k, (bk,) = misc.take()
                        for c in range(C2):
                            nc.tensor.matmul(bank(bk)[:, 0:2 * N], xT[:, i % 2, c, :], wbc[:, c, :], start=(c == 0), stop=(c == C2 - 1))
                        for h in range(2):
                            for c in range(C2):
                                last = nc.tensor.matmul(bank(bk)[0:N, (1 + h) * P:(2 + h) * P], wbc[:, c, h * N:(h + 1) * N],
                                                        xT[:, i % 2, c, :], start=(c == 0), stop=(c == C2 - 1))
                        pt["bc_made", i] = PE.op(last)
                        A.wait(pt["bc_made", i], pt.get(("pe_back", i - 3)), pt.get(("bc_read", i - 3)))
                        A.op(nc.scalar.copy(bctok[:, s, :], bank(bk)[:, 0:2 * N]))
                        pt["bc", i] = A.op(nc.scalar.copy(bct[:, s], bank(bk)[0:N, P:3 * P].rearrange("p (c t) -> p c t", c=2)))
                        misc.release(k, pt["bc", i])

                    def chunk_pairs(i):
                        s = i % 3
                        PE.wait(pt["bc", i])
                        k, (bk,) = misc.take()
                        gp = PE.op(nc.tensor.matmul(bank(bk)[:, 0:P], bct[:, s, 0, :], bct[:, s, 1, :], start=True, stop=True))
                        V.wait(gp, pt.get(("pe_back", i - 3)))
                        p = V.op(nc.vector.tensor_tensor(gm[:, s], wide(bank(bk)[:, 0:P].rearrange("p (o n) -> p o n", o=1), 1, NEG_LOG),
                                                         pairs[:, :, :], ALU.mult))
                        misc.release(k, p)
                        pt["gm", i] = p
                        V.wait(pt["bc", i], pt.get(("bc_read", i - 1)))
                        pt["bc_read", i] = V.op(nc.vector.tensor_tensor_reduce(gjunk[:, :], bctok[:, s, 0:N], bctok[:, s, N:2 * N], 1.0, 0.0,
                                                                               ALU.mult, ALU.add, gtt[:, s, :]))

                    def chunk_mix(i):
                        s, r = i % 2, i % 3
                        PE.wait(pt["val", i], pt["gm", i], yfree[0], pt.get(("state", i - 1)))
                        for l in range(NEG_LOG):
                            nc.tensor.matmul(bank(4 + l // 2)[:, (l % 2) * DI:(l % 2 + 1) * DI], gm[:, r, l, :], val[:, s, l, :],
                                             start=True, stop=True)
                        yp = PE.op(nc.tensor.matmul(bank(7)[:, DI:2 * DI], bct[:, r, 1, :], state[:, :], start=True, stop=True))
                        k, (bk,) = misc.take()
                        hp = PE.op(nc.tensor.matmul(bank(bk)[0:N, 0:DI], bctok[:, r, 0:N], val[:, s, 7, :], start=True, stop=True))
                        pt["pe_back", i] = hp
                        V.wait(yp, pt["decays", i], pt.get(("y_read", i - 1)))
                        V.op(nc.vector.tensor_tensor(zz[:, 0:7, :], psum[:, 4:8, :].rearrange("p b (l n) -> p (b l) n", l=2)[:, 0:7, :],
                                                     dec[:, s, 0:7, :], ALU.mult))
                        V.op(nc.vector.tensor_tensor(zz[:, 7, :], bank(7)[:, DI:2 * DI], dec[:, s, 8, :], ALU.mult))
                        yfree[0] = pt["z_read", i] = V.now()
                        V.step(nc.vector.tensor_tensor(state[:, :], state[:, :], total[:, s, :], ALU.mult))
                        V.wait(hp)
                        p = V.op(nc.vector.tensor_tensor(state[:, :], state[:, :], bank(bk)[0:N, 0:DI], ALU.add))
                        pt["state", i] = p
                        misc.release(k, p)
                        V.wait(pt["z_read", i], pt.get(("y_turned", i - 1)))
                        V.op(nc.vector.tensor_reduce(yy[:, :], zz[:, :, :].rearrange("p l n -> p n l"), X, ALU.add))
                        V.wait(pt["skip", i])
                        V.step(nc.vector.scalar_tensor_tensor(skip[:, s, :], dtx[:, i, :], gtt[:, r, :], skip[:, s, :], ALU.mult, ALU.add))
                        V.step(nc.vector.tensor_tensor(yy[:, :], yy[:, :], skip[:, s, :], ALU.add))
                        pt["y_read", i] = V.step(nc.vector.tensor_tensor(yy[:, :], yy[:, :], xz[:, i, DI:2 * DI], ALU.mult))

                    def chunk_y_turn(i):
                        PE.wait(pt["y_read", i])
                        k, (bk,) = misc.take()
                        for c in range(C2):
                            last = nc.tensor.transpose(bank(bk)[:, c * P:(c + 1) * P], yy[:, c * P:(c + 1) * P], ident[:, :])
                        tp = PE.op(last)
                        pt["y_turned", i] = tp
                        A.wait(tp, pt.get(("yT_read", i - 1)))
                        yr = pt["yT", i] = A.op(nc.scalar.copy(yT[:, :, :], bank(bk)[:, 0:C2 * P].rearrange("p (c t) -> p c t", c=C2)))
                        misc.release(k, yr)

                    def chunk_out(i):
                        PE.wait(pt["yT", i])
                        k, (bk,) = misc.take()
                        for c in range(C2):
                            last = nc.tensor.matmul(bank(bk)[:, 0:D], yT[:, c, :], wout[:, c, :], start=(c == 0), stop=(c == C2 - 1))
                        op = PE.op(last)
                        pt["yT_read", i] = op
                        V.wait(op)
                        h = hid[:, b * NT + i, :]
                        p = V.op(nc.vector.scalar_tensor_tensor(h, bank(bk)[:, 0:D], mask[:, b, 0:1], h, ALU.mult, ALU.add))
                        misc.release(k, p)

                    for i in range(2):
                        chunk_turn(i)
                        chunk_bc(i)
                        chunk_pairs(i)
                    for j in range(5):
                        chunk_front(0, j)
                    for i in range(NT):
                        chunk_mix(i)
                        for j in range(5):
                            if i + 1 < NT:
                                chunk_front(i + 1, j)
                            if i + 2 < NT and j == 0:
                                chunk_turn(i + 2)
                            if i + 2 < NT and j == 3:
                                chunk_bc(i + 2)
                        chunk_y_turn(i)
                        if i + 2 < NT:
                            chunk_pairs(i + 2)
                        chunk_out(i)
                    barrier()

        def phase_T():
            with ExitStack() as st:
                w = sb(st, "tc_w", [P, D])
                bias = sb(st, "tc_b", [1, D])
                th = sb(st, "tc_theta", [P, 1])
                turn = sb(st, "tc_turn", [P, 1])
                cs = sb(st, "tc_cos_sin", [P, 2])
                tanh = sb(st, "tc_tanh", [P, NT, D])
                mixed = sb(st, "tc_mixed", [P, NT, D])
                ld = new_loads("tc_loads")
                ld.start(w[:, :], a["tc_w"])
                ld.start(bias[:, :], a["tc_b"].rearrange("(o n) -> o n", o=1))
                ld.start(th[:, :], wide(a["tc_theta"].rearrange("(o n) -> o n", o=1), 0, P))
                V.wait(ld.now()); PE.wait(ld.now())
                BIG = float(1.5 * 2 ** 23)
                V.step(nc.vector.tensor_scalar(turn[:, :], th[:, :], float(1 / (2 * np.pi)), BIG, ALU.mult, ALU.add))
                V.step(nc.vector.tensor_scalar(turn[:, :], turn[:, :], BIG, None, ALU.subtract))
                tau_hi = float(np.float32(6.28125))
                tau_lo = float(2 * np.pi - 6.28125)
                V.step(nc.vector.scalar_tensor_tensor(th[:, :], turn[:, :], -tau_hi, th[:, :], ALU.mult, ALU.add))
                V.step(nc.vector.scalar_tensor_tensor(th[:, :], turn[:, :], -tau_lo, th[:, :], ALU.mult, ALU.add))
                V.step(nc.vector.tensor_scalar(th[:, :], th[:, :], float(np.float32(np.pi)), -float(np.float32(np.pi)), ALU.min, ALU.max))
                V.step(nc.vector.scalar_tensor_tensor(turn[:, :], th[:, :], -1.0, th[:, :], ALU.mult, ALU.max))
                V.step(nc.vector.tensor_scalar(turn[:, :], turn[:, :], -1.0, float(np.pi / 2), ALU.mult, ALU.add))
                A.wait(V.now())
                A.op(nc.scalar.activation(cs[:, 0:1], turn[:, :], ACT.Sin))
                A.op(nc.scalar.activation(cs[:, 1:2], th[:, :], ACT.Sin))
                V.wait(A.now())
                for b in range(NB):
                    ring = Ring(PE, [(k,) for k in range(8)])
                    done = to_channels(ring, norm, layernorm(hid, norm[:, :, :], b, 1e-6, 1), b)
                    PE.wait(*done)
                    for g in range(NT // 4):
                        k, (bk,) = ring.take()
                        for q in range(4):
                            o = bank(bk)[:, q * D:(q + 1) * D]
                            nc.tensor.matmul(o, chans[:, b, PAD + (4 * g + q) * P:PAD + (4 * g + q + 1) * P], w[:, :], start=True, stop=False)
                            last = nc.tensor.matmul(o, ones[0:1, :], bias[:, :], start=False, stop=True)
                        A.wait(PE.op(last))
                        p = A.op(nc.scalar.activation(tanh[:, 4 * g:4 * g + 4, :], bank(bk).rearrange("p (q n) -> p q n", q=4), ACT.Tanh))
                        ring.release(k, p)
                    V.step(nc.vector.tensor_scalar(mixed[:, :, :], norm[:, :, :], cs[:, 0:1], None, ALU.mult))
                    V.wait(A.now())
                    V.step(nc.vector.scalar_tensor_tensor(mixed[:, :, :], tanh[:, :, :], cs[:, 1:2], mixed[:, :, :], ALU.mult, ALU.add))
                    h = hid[:, b * NT:(b + 1) * NT, :]
                    V.step(nc.vector.scalar_tensor_tensor(h, mixed[:, :, :], mask[:, b, 1:2], h, ALU.mult, ALU.add))
                    barrier()

        NG, HD, NH, ROWS = 9, 8, 16, 96

        def phase_C():
            B2 = S // 2
            CT = B2 // P
            HB = NH // 4
            MR = NG * HD
            INV = 0.7071067811865476
            SC = 1.0 / float(np.sqrt(HD))
            with ExitStack() as st:
                wqkv = sb(st, "w_qkv", [P, 3 * D])
                wo = sb(st, "w_o", [P, D])
                cw = sb(st, "wlam_conv", [P, 4])
                ld = new_loads("wlam_loads")
                for j, n in enumerate(("w_q", "w_k", "w_v")):
                    ld.start(wqkv[:, j * D:(j + 1) * D], a[n])
                ld.start(wo[:, :], a["w_o"])
                with nc.allow_non_contiguous_dma("4 taps a channel"):
                    ld.start(cw[:, :], a["wlam_conv"].rearrange("k d -> d k"))
                aT = sb(st, "wl_sum", [P, B2])
                dT = sb(st, "wl_diff", [P, B2])
                qf = sb(st, "wl_q", [P, 4, 2 * D])
                part = sb(st, "wl_parts", [P, 3, 4, 2 * D], BF16)
                uq = sb(st, "wl_q_rows", [P, CT, NH, ROWS], BF16)
                uk = sb(st, "wl_k_rows", [P, CT, NH, ROWS], BF16)
                qT = sb(st, "wl_qT", [ROWS, 8, B2], BF16)
                kT = sb(st, "wl_kT", [ROWS, 8, B2], BF16)
                vp = sb(st, "wl_v", [P, CT, NH, 32])
                negm = sb(st, "wl_negmax", [P, CT, NH])
                mrest = sb(st, "wl_negmax_rest", [P, CT, 4])
                prob = sb(st, "wl_p", [P, 3, 2 * BANK])
                oc = sb(st, "wl_oT", [P, 2 * BANK])
                rr = sb(st, "wl_recip", [P, CT, 4])
                otok = sb(st, "wl_o", [P, CT, D])
                oT = aT
                yp = sb(st, "wl_y", [P, S + 4])
                chs = cv = norm[:, :, :].rearrange("p i n -> p (i n)")
                first_norm = layernorm(hid, norm[:, :, :], 0, 1e-6, 2)
                for e in (PE, V, A, G):
                    e.wait(ld.now())
                V.op(nc.vector.memset(yp[:, :], 0.0))
                G.op(nc.gpsimd.memset(vp[:, :, :, :], 0.0))
                G.op(nc.gpsimd.memset(uq[:, :, :, MR:ROWS], 0.0))
                G.op(nc.gpsimd.memset(uk[:, :, :, MR:ROWS], 0.0))
                G.wait(G.now())
                G.op(nc.gpsimd.memset(vp[:, :, :, HD:HD + 1], 1.0))
                G.op(nc.gpsimd.memset(uk[:, :, :, MR:MR + 3], 1.0))
                for b in range(NB):
                    ring = Ring(PE, [(k,) for k in range(8)])
                    done = to_channels(ring, norm, layernorm(hid, norm[:, :, :], b, 1e-6, 2) if b else first_norm, b)
                    V.wait(*done)
                    V.wait(PE.now())
                    V.step(nc.vector.tensor_scalar(chs[:, :], chans[:, b, PAD:PAD + S], INV, None, ALU.mult))
                    eo = chs[:, :].rearrange("p (t e) -> p t e", e=2)
                    V.op(nc.vector.tensor_tensor(aT[:, :], eo[:, :, 0], eo[:, :, 1], ALU.add))
                    PE.wait(V.now())
                    V.op(nc.vector.tensor_tensor(dT[:, :], eo[:, :, 0], eo[:, :, 1], ALU.subtract))
                    if b:
                        G.op(nc.gpsimd.memset(uq[:, :, :, MR:MR + 3], 0.0))
                    A.wait(G.now())
                    spread_done = ()
                    for g in range(CT // 4):
                        A.wait(*spread_done)
                        for q in range(4):
                            i = 4 * g + q
                            k, (bk,) = ring.take()
                            A.wait(PE.op(nc.tensor.matmul(bank(bk)[:, 0:3 * D], aT[:, i * P:(i + 1) * P], wqkv[:, :], start=True, stop=True)))
                            A.op(nc.scalar.copy(qf[:, q, :], bank(bk)[:, 0:2 * D]))
                            p = A.op(nc.scalar.copy(vp[:, i, :, 0:HD], bank(bk)[:, 2 * D:3 * D].rearrange("p (h x) -> p h x", x=HD)))
                            ring.release(k, p)
                        V.wait(p, *spread_done)
                        points = []
                        for n in range(3):
                            if n:
                                V.step(nc.vector.tensor_tensor(qf[:, :, :], qf[:, :, :], part[:, n - 1], ALU.subtract))
                            points.append(V.step(nc.vector.tensor_copy(part[:, n], qf[:, :, :])))
                        ts_ = slice(4 * g, 4 * g + 4)
                        j = 0
                        for n in range(3):
                            for u, c0 in ((uq, 0), (uk, D)):
                                rows = u[:, ts_, :, 0:MR].rearrange("p t h (i j x) -> p t h i j x", i=3, j=3)
                                src8 = part[:, n, :, c0:c0 + D].rearrange("p t (h x) -> p t h x", x=HD)
                                for c in range(3):
                                    o = rows[:, :, :, n, c, :] if c0 == 0 else rows[:, :, :, c, n, :]
                                    e = (V, A, G, V, A, V)[j % 6]
                                    j += 1
                                    e.wait(points[n])
                                    if e is V:
                                        V.op(nc.vector.tensor_copy(o, src8))
                                    elif e is A:
                                        A.op(nc.scalar.copy(o, src8))
                                    else:
                                        G.op(nc.gpsimd.tensor_copy(o, src8))
                        spread_done = (V.now(), A.now(), G.now())
                    PE.wait(*spread_done)

                    sr = Ring(PE, [(0, 1), (2, 3), (4, 5)])
                    orr = Ring(PE, [(6, 7)])
                    pt = {}
                    pfree = [None] * 3
                    slots = [0]
                    both = ((uq, qT), (uk, kT))

                    def head_rows(pairs, h):
                        k, bks = sr.take()
                        for (u, dst), bk in zip(pairs, bks):
                            bv = psum[0:ROWS, bk, :].bitcast(BF16)
                            for q in range(CT):
                                last = nc.tensor.transpose(bv[:, q * P:(q + 1) * P], u[:, q, h, :], identb[:, :])
                            A.wait(PE.op(last))
                            p = A.op(nc.scalar.copy(dst[:, h % 8, :], bv))
                        sr.release(k, p)
                        return p

                    def maxima(g):
                        for h in range(4 * g, 4 * g + 4):
                            if ("rows", h) not in pt:
                                pt["rows", h] = head_rows(both, h)
                            for i in range(CT):
                                if i == 0:
                                    PE.wait(pt["rows", h])
                                if i == 5 and h % 4 < 3:
                                    pt["rows", h + 1] = head_rows(both, h + 1)
                                k, bks = sr.take()
                                for j in range(B2 // BANK):
                                    last = nc.tensor.matmul(bank(bks[j]), qT[:, h % 8, i * P:(i + 1) * P], kT[:, h % 8, j * BANK:(j + 1) * BANK],
                                                            start=True, stop=True)
                                V.wait(PE.op(last))
                                p = V.op(nc.vector.tensor_reduce(negm[:, i, h:h + 1], psum[:, bks[0]:bks[0] + 2, :].rearrange("p b n -> p (b n)"),
                                                                 X, ALU.max, negate=True))
                                sr.release(k, p)
                                pt["max", g] = p
                                yield

                    def max_rows(g):
                        hs = slice(4 * g, 4 * g + 4)
                        V.wait(pt["max", g])
                        V.step(nc.vector.tensor_copy(mrest[:, :, :], negm[:, :, hs]))
                        for n in range(3):
                            p = V.step(nc.vector.tensor_copy(uq[:, :, hs, MR + n], mrest[:, :, :]))
                            if n < 2:
                                V.step(nc.vector.tensor_tensor(mrest[:, :, :], mrest[:, :, :], uq[:, :, hs, MR + n], ALU.subtract))
                        PE.wait(p)
                        for h in range(4 * g, 4 * g + 4):
                            pt["q", g] = head_rows(both[:1], h)

                    def attend(g):
                        PE.wait(pt["q", g])
                        ko, (o0, o1) = orr.take()
                        pend = []

                        def av(item):
                            kt, hh, slot, ep = item
                            PE.wait(ep)
                            for j in range(2):
                                last = nc.tensor.matmul(bank((o0, o1)[j])[32 * hh:32 * hh + 32, :], vp[:, kt, 4 * g + hh, :],
                                                        prob[:, slot, j * BANK:(j + 1) * BANK], start=(kt == 0), stop=(kt == CT - 1),
                                                        skip_group_check=True, tile_position=(0, 32 * hh))
                            pfree[slot] = PE.op(last)
                        for kt in range(CT):
                            for hh in range(4):
                                k, bks = sr.take()
                                for j in range(2):
                                    last = nc.tensor.matmul(bank(bks[j]), kT[:, (4 * g + hh) % 8, kt * P:(kt + 1) * P],
                                                            qT[:, (4 * g + hh) % 8, j * BANK:(j + 1) * BANK], start=True, stop=True)
                                slot = slots[0] % 3
                                slots[0] += 1
                                A.wait(PE.op(last), pfree[slot])
                                p = A.op(nc.scalar.activation(prob[:, slot, :], psum[:, bks[0]:bks[0] + 2, :].rearrange("p b n -> p (b n)"),
                                                              ACT.Exp, scale=SC))
                                sr.release(k, p)
                                pend.append((kt, hh, slot, p))
                                if len(pend) > 2:
                                    av(pend.pop(0))
                                yield
                        while pend:
                            av(pend.pop(0))
                        V.wait(PE.now(), pt.get(("oc", g - 1)))
                        c = V.op(nc.vector.tensor_copy(oc[:, :], psum[:, o0:o0 + 2, :].rearrange("p b n -> p (b n)")))
                        orr.release(ko, c)
                        pt["o", g] = c

                    def normalise(g):
                        PE.wait(pt["o", g])
                        k, bks = sr.take()
                        for q4, bk in zip(range(CT // 4), bks):
                            for q in range(4):
                                t = 4 * q4 + q
                                last = nc.tensor.transpose(bank(bk)[:, q * P:(q + 1) * P], oc[:, t * P:(t + 1) * P], ident[:, :])
                            pt["oc", g] = PE.op(last)
                            V.wait(pt["oc", g])
                            v4 = bank(bk).rearrange("p (q h x) -> p q h x", q=4, h=4)
                            V.step(nc.vector.reciprocal(rr[:, 4 * q4:4 * q4 + 4, :], v4[:, :, :, HD]))
                            for q in range(4):
                                p = V.op(nc.vector.tensor_tensor(
                                    otok[:, 4 * q4 + q, 32 * g:32 * g + 32].rearrange("p (h x) -> p h x", x=HD), v4[:, q, :, 0:HD],
                                    wide(rr[:, 4 * q4 + q, :].rearrange("p (h o) -> p h o", o=1), 2, HD), ALU.mult))
                        sr.release(k, p)

                    PE.wait(V.now(), A.now())
                    for _ in maxima(0):
                        pass
                    for g in range(HB):
                        max_rows(g)
                        second, first_ = attend(g), maxima(g + 1) if g + 1 < HB else iter(())
                        if g + 1 < HB:
                            pt["rows", 4 * g + 4] = head_rows(both, 4 * g + 4)
                        n = 0
                        for _ in second:
                            next(first_, None)
                            n += 1
                            if n == 6 and g:
                                normalise(g - 1)
                        for _ in first_:
                            pass
                    normalise(HB - 1)
                    barrier()
                    ring = Ring(PE, [(k,) for k in range(8)])
                    done = to_channels(ring, otok, V.now(), b, CT, oT, 0)
                    PE.wait(*done)
                    yv = yp[:, 2:2 + S].rearrange("p (t e) -> p t e", e=2)
                    for j in range(B2 // BANK):
                        k, (bk,) = ring.take()
                        V.wait(PE.op(nc.tensor.matmul(bank(bk), wo[:, :], oT[:, j * BANK:(j + 1) * BANK], start=True, stop=True)))
                        dj = dT[:, j * BANK:(j + 1) * BANK]
                        V.op(nc.vector.tensor_tensor(yv[:, j * BANK:(j + 1) * BANK, 0], bank(bk), dj, ALU.add))
                        p = V.op(nc.vector.tensor_tensor(yv[:, j * BANK:(j + 1) * BANK, 1], bank(bk), dj, ALU.subtract))
                        ring.release(k, p)
                    V.wait(V.now())
                    V.step(nc.vector.tensor_scalar(yp[:, 2:2 + S], yp[:, 2:2 + S], INV, None, ALU.mult))
                    V.step(nc.vector.tensor_scalar(cv[:, :], yp[:, 0:S], cw[:, 0:1], None, ALU.mult))
                    for c in range(1, 4):
                        V.step(nc.vector.scalar_tensor_tensor(cv[:, :], yp[:, c:c + S], cw[:, c:c + 1], cv[:, :], ALU.mult, ALU.add))
                    PE.wait(V.now())
                    for g in range(NT // 4):
                        k, (bk,) = ring.take()
                        for q in range(4):
                            t = 4 * g + q
                            last = nc.tensor.transpose(bank(bk)[:, q * P:(q + 1) * P], cv[:, t * P:(t + 1) * P], ident[:, :])
                        V.wait(PE.op(last))
                        h = hid[:, b * NT + 4 * g:b * NT + 4 * g + 4, :]
                        p = V.op(nc.vector.scalar_tensor_tensor(h, bank(bk).rearrange("p (q n) -> p q n", q=4), mask[:, b, 2:3], h,
                                                                ALU.mult, ALU.add))
                        ring.release(k, p)
                    barrier()

        def phase_D():
            E_, _, FF = a["moe_w1"].shape
            FT = FF // P
            with ExitStack() as st:
                w1 = sb(st, "moe_w1", [P, E_, FF])
                w2 = sb(st, "moe_w2", [P, E_ * FT, D])
                b1 = sb(st, "moe_b1", [P, E_ * FT])
                b2 = sb(st, "moe_b2", [1, E_, D])
                wg = sb(st, "moe_wg", [P, E_])
                before = sb(st, "moe_before", [P, E_ * E_])
                ld = new_loads("moe_loads")
                ld.start(wg[:, :], a["moe_wg"])
                ld.start(before[:, :], a["c_before8"])
                with nc.allow_non_contiguous_dma("one bias per channel"):
                    ld.start(b1[:, :], a["moe_b1"].rearrange("e (f p) -> p (e f)", p=P))
                ld.start(b2[:, :, :], a["moe_b2"].rearrange("(o e) d -> o e d", o=1))
                ldw = new_loads("moe_weight_loads")
                for e in range(E_):
                    ldw.start(w1[:, e, :], a["moe_w1"][e])
                ldw.start(w2[:, :, :], a["moe_w2"].rearrange("e (f p) d -> p (e f) d", p=P))
                lg = sb(st, "moe_logits", [P, NT, E_])
                gates = sb(st, "moe_gates", [P, NB, NT, E_])
                cmp_ = sb(st, "moe_cmp", [P, NT, E_ * E_])
                eq = sb(st, "moe_eq", [P, NT, E_ * E_])
                mx = sb(st, "moe_max", [P, NT])
                hbuf = sb(st, "moe_h", [P, 2, FT, BANK])
                acc = sb(st, "moe_acc", [P, NT, D])
                r1 = Ring(PE, [(0,), (1,), (2,), (3,)])
                r2 = Ring(PE, [(4,), (5,), (6,), (7,)])

                def route(b):
                    gt = gates[:, b]
                    yield from layernorm_steps(hid, norm[:, :, :], b, 1e-6, 3)
                    yield from to_channels_steps(r2, norm, V.now(), b)
                    PE.wait(A.now(), V.now())
                    k, (bk,) = r2.take()
                    for i in range(NT):
                        last = nc.tensor.matmul(bank(bk)[:, i * E_:(i + 1) * E_], chans[:, b, PAD + i * P:PAD + (i + 1) * P], wg[:, :],
                                                start=True, stop=True)
                    V.wait(PE.op(last))
                    V.step(nc.vector.tensor_copy(lg[:, :, :], bank(bk)[:, 0:NT * E_].rearrange("p (i e) -> p i e", e=E_)))
                    r2.release(k, V.now())
                    yield
                    mine = wide(lg[:, :, :].rearrange("p i (e o) -> p i e o", o=1), 3, E_)
                    other = wide(lg[:, :, :].rearrange("p i (o e) -> p i o e", o=1), 2, E_)
                    sq = lambda t: t[:, :, :].rearrange("p i (e o) -> p i e o", o=E_)
                    V.op(nc.vector.tensor_tensor(sq(cmp_), other, mine, ALU.is_gt))
                    V.step(nc.vector.tensor_tensor(sq(eq), other, mine, ALU.is_equal))
                    yield
                    V.step(nc.vector.tensor_tensor(eq[:, :, :], eq[:, :, :], wide(before[:, :].rearrange("p (o n) -> p o n", o=1), 1, NT), ALU.mult))
                    yield
                    V.step(nc.vector.tensor_tensor(cmp_[:, :, :], cmp_[:, :, :], eq[:, :, :], ALU.add))
                    yield
                    V.op(nc.vector.tensor_reduce(gt[:, :, :], sq(cmp_), X, ALU.add))
                    V.step(nc.vector.tensor_reduce(mx[:, :], lg[:, :, :], X, ALU.max))
                    V.step(nc.vector.tensor_scalar(gt[:, :, :], gt[:, :, :], 2.0, None, ALU.is_lt))
                    col = lambda t: wide(t[:, :].rearrange("p (i o) -> p i o", o=1), 2, E_)
                    V.step(nc.vector.tensor_tensor(lg[:, :, :], lg[:, :, :], col(mx), ALU.subtract))
                    yield
                    A.wait(V.now())
                    p = A.op(nc.scalar.activation(lg[:, :, :], lg[:, :, :], ACT.Exp))
                    yield
                    V.wait(p)
                    V.step(nc.vector.tensor_tensor(gt[:, :, :], gt[:, :, :], lg[:, :, :], ALU.mult))
                    yield
                    V.step(nc.vector.tensor_reduce(mx[:, :], gt[:, :, :], X, ALU.add))
                    V.step(nc.vector.reciprocal(mx[:, :], mx[:, :]))
                    V.step(nc.vector.tensor_tensor(gt[:, :, :], gt[:, :, :], col(mx), ALU.mult))
                    yield
                    V.step(nc.vector.tensor_scalar(gt[:, :, :], gt[:, :, :], mask[:, b, 3:4], None, ALU.mult))

                hread = [None, None]
                pend = []
                added = {}

                def down(item):
                    b, g, e, s, ready = item
                    PE.wait(ready)
                    k, (bk,) = r2.take()
                    for q in range(4):
                        o = bank(bk)[:, q * D:(q + 1) * D]
                        for f in range(FT):
                            nc.tensor.matmul(o, hbuf[:, s, f, q * P:(q + 1) * P], w2[:, e * FT + f, :], start=(f == 0), stop=False)
                        last = nc.tensor.matmul(o, ones[0:1, :], b2[:, e, :], start=False, stop=True)
                    p = PE.op(last)
                    V.wait(p)
                    for q in range(4):
                        t = 4 * g + q
                        h = hid[:, b * NT + t, :]
                        V.wait(added.get((b, t)))
                        v = added[b, t] = V.op(nc.vector.scalar_tensor_tensor(h, bank(bk)[:, q * D:(q + 1) * D], gates[:, b, t, e:e + 1], h,
                                                                              ALU.mult, ALU.add))
                    r2.release(k, v)
                    return p

                def residual(b):
                    V.wait(V.now())
                    x = res[:, b * NT:(b + 1) * NT, :]
                    V.op(nc.vector.tensor_tensor(x, x, hid[:, b * NT:(b + 1) * NT, :], ALU.add))

                steps = route(0)
                for _ in range(NT // 2 + 2):
                    next(steps)
                for e in (PE, V, A, G):
                    e.wait(ld.now())
                for _ in steps:
                    pass
                PE.wait(ldw.now(), V.now(), A.now())
                n = 0
                for b in range(NB):
                    beside = route(b + 1) if b + 1 < NB else iter(())
                    for g in range(NT // 4):
                        for e in range(E_):
                            s = n % 2
                            n += 1
                            for f in range(FT):
                                k, (bk,) = r1.take()
                                p = PE.op(nc.tensor.matmul(bank(bk), w1[:, e, f * P:(f + 1) * P],
                                                           chans[:, b, PAD + g * BANK:PAD + (g + 1) * BANK], start=True, stop=True))
                                A.wait(p, hread[s])
                                p = A.op(nc.scalar.activation(hbuf[:, s, f, :], bank(bk), ACT.Gelu_apprx_tanh,
                                                              bias=b1[:, e * FT + f:e * FT + f + 1]))
                                r1.release(k, p)
                            pend.append((b, g, e, s, p))
                            if len(pend) > 1:
                                it = pend.pop(0)
                                hread[it[3]] = down(it)
                            for _ in range(2):
                                next(beside, None)
                    for _ in beside:
                        pass
                    while pend:
                        down(pend.pop(0))
                    residual(b)
                barrier()

        def phase_E(tag):
            NHE, HDE, NA = 16, 64, 4
            NPAIR = NA // 2
            QC = S // BANK
            with ExitStack() as st:
                def buf(name, shp, dt=F32):
                    return sb(st, "f_" + name + tag, shp, dt)

                wr = buf("wr", [P, NHE])
                br = buf("br", [1, NHE])
                wo = buf("wo", [P, NPAIR, D])
                bo = buf("bo", [P, D])
                before = buf("before", [1, NHE * NHE])
                index = buf("index", [1, NHE])
                ld = new_loads("ffn_loads" + tag)
                ld.start(wr[:, :], a["Wr"])
                ld.start(br[:, :], a["br"].rearrange("(o n) -> o n", o=1))
                ld.start(wo[:, :, :], a["Wo"].rearrange("(j p) d -> p j d", p=P))
                ld.start(bo[:, :], bcast(a["bo"], P))
                ld.start(before[:, :], a["c_before"][0:1, :])
                ld.start(index[:, :], a["c_index"][0:1, :])
                sels = [[new_loads(f"ffn_heads{tag}_{b}_{jp}") for jp in range(NPAIR)] for b in range(NB)]
                ws = buf("wqk", [P, NB, 2, NA, 2, HDE])
                wv = buf("wv", [P, NB, NA, HDE])
                bqk = buf("bqk", [P, NB, 2, NA])
                bv = buf("bv", [P, NB, NA, HDE])
                pooled = buf("pooled", [P, 1])
                d = buf("dist", [1, NHE])
                sc = buf("sc", [1, 2])
                rank = buf("rank", [1, NHE])
                pos = buf("pos", [1, NHE])
                idf = buf("idf", [1, NA])
                idi = buf("idi", [1, NB, NA], I32)
                qhh, qmm, qhl, khm, klh = (buf(n, [P, 2, 2, S], BF16) for n in ("qhh", "qmm", "qhl", "khm", "klh"))
                vt = buf("v", [P, 2, NT, 2, HDE])
                pT = buf("pT", [P, 4, NT, P])
                pb = hid[:, :, :].rearrange("p (s i) n -> p s (i n)", s=2)
                cm, eq = (norm[0:1, 2 * n:2 * n + 2, :].rearrange("p a n -> p (a n)").rearrange("p (h o) -> p h o", o=NHE) for n in range(2))
                q32 = norm[:, 0:12, :].rearrange("p (s i) n -> p s (i n)", s=3)
                parts = norm[:, 12:16, :].rearrange("p i n -> p (i n)").bitcast(BF16).rearrange("p (a n) -> p a n", a=2)
                m2 = buf("m2", [P, 4, 2])
                nm = buf("nm", [P, 4])
                rs = buf("rs", [P, 8, 2])
                oT = buf("oT", [P, 2, P])

                def choose(b, ring):
                    yield from layernorm_steps(res, norm[:, :, :], b, 1e-5)
                    yield from to_channels_steps(ring, norm, V.now(), b)
                    done = (A.now(), V.now())
                    V.wait(*done)
                    V.step(nc.vector.tensor_reduce(pooled[:, :], chans[:, b, PAD:PAD + S], X, ALU.add))
                    yield
                    p = V.step(nc.vector.tensor_scalar(pooled[:, :], pooled[:, :], 1.0 / S, None, ALU.mult))
                    PE.wait(p, *done)
                    k, (bk,) = ring.take()
                    V.wait(PE.op(nc.tensor.matmul(bank(bk)[0:1, 0:NHE], pooled[:, :], wr[:, :], start=True, stop=True)))
                    V.step(nc.vector.tensor_tensor(d[:, :], bank(bk)[0:1, 0:NHE], br[:, :], ALU.add))
                    ring.release(k, V.now())
                    yield
                    V.step(nc.vector.tensor_reduce(sc[:, 0:1], d[:, :], X, ALU.max, negate=True))
                    yield
                    A.wait(V.now())
                    p = A.op(nc.scalar.activation(d[:, :], d[:, :], ACT.Exp, bias=sc[:, 0:1]))
                    V.wait(p)
                    V.step(nc.vector.tensor_reduce(sc[:, 1:2], d[:, :], X, ALU.add))
                    yield
                    V.step(nc.vector.reciprocal(sc[:, 1:2], sc[:, 1:2]))
                    yield
                    V.step(nc.vector.tensor_scalar(d[:, :], d[:, :], sc[:, 1:2], None, ALU.mult))
                    yield
                    mine = wide(d[:, :].rearrange("p (h o) -> p h o", o=1), 2, NHE)
                    other = wide(d[:, :].rearrange("p (o h) -> p o h", o=1), 1, NHE)
                    bf = before[:, :].rearrange("p (h o) -> p h o", o=NHE)
                    V.op(nc.vector.tensor_tensor(cm, other, mine, ALU.is_gt))
                    V.step(nc.vector.tensor_tensor(eq, other, mine, ALU.is_equal))
                    yield
                    V.step(nc.vector.tensor_tensor(eq, eq, bf, ALU.mult))
                    yield
                    V.step(nc.vector.tensor_tensor(cm, cm, eq, ALU.add))
                    yield
                    V.step(nc.vector.tensor_reduce(rank[:, :], cm, X, ALU.add))
                    yield
                    V.step(nc.vector.tensor_scalar(rank[:, :], rank[:, :], float(NA), None, ALU.is_lt))
                    yield
                    V.step(nc.vector.tensor_tensor(cm, wide(rank[:, :].rearrange("p (o h) -> p o h", o=1), 1, NHE), bf, ALU.mult))
                    yield
                    V.step(nc.vector.tensor_reduce(pos[:, :], cm, X, ALU.add))
                    yield
                    for j in range(NA):
                        V.step(nc.vector.scalar_tensor_tensor(eq[:, j, :], pos[:, :], float(j), rank[:, :], ALU.is_equal, ALU.mult))
                        V.step(nc.vector.tensor_tensor(eq[:, j, :], eq[:, j, :], index[:, :], ALU.mult))
                        yield
                    V.step(nc.vector.tensor_reduce(idf[:, :], eq[:, 0:NA, :], X, ALU.add))
                    yield
                    V.step(nc.vector.tensor_copy(idi[:, b, :], idf[:, :]))
                    yield
                    pt["norm_free"] = (PE.now(), V.now())
                    SP.wait(V.now())
                    for j in range(NA):
                        sel = sels[b][j // 2]
                        hsel = nc.sync.value_load(idi[0:1, b, j:j + 1], min_val=0, max_val=NHE - 1)
                        at = bass.ds(hsel * HDE, HDE)
                        for n, name in enumerate(("Wq", "Wk")):
                            sel.start(ws[:, b, n, j, :, :], wide(a[name][:, at].rearrange("p (o x) -> p o x", o=1), 1, 2))
                        with nc.allow_non_contiguous_dma("one bias per channel"):
                            for n, name in enumerate(("bq", "bk")):
                                for r in range(2):
                                    sel.start(bqk[64 * r:64 * r + 64, b, n, j:j + 1], a[name][at].rearrange("(p o) -> p o", o=1))
                        sel.start(wv[:, b, j, :], a["Wv"][:, at])
                        sel.start(bv[:, b, j, :], wide(a["bv"][at].rearrange("(o n) -> o n", o=1), 0, P))
                    G.wait(V.now())
                    x = res[:, b * NT:(b + 1) * NT, :]
                    pt["bias", b] = G.op(nc.gpsimd.tensor_tensor(x, x, wide(bo[:, :].rearrange("p (o n) -> p o n", o=1), 1, NT), ALU.add))

                pt = {}
                steps = choose(0, Ring(PE, [(k,) for k in range(8)]))
                for _ in range(NT // 2 + 2):
                    next(steps)
                for e in (PE, V, A, G, SP):
                    e.wait(ld.now())
                for _ in steps:
                    pass
                PE.wait(V.now(), A.now())

                pairs_ = [(b, jp) for b in range(NB) for jp in range(NPAIR)]
                units = [(n, i, h) for n in range(len(pairs_)) for i in range(NT) for h in range(2)]
                NU = len(units)
                SC = 1.0 / float(np.sqrt(HDE))
                sr = Ring(PE, [(0, 1), (2, 3)])
                tr = Ring(PE, [(4,), (5,)])
                orr = Ring(PE, [(6,)])
                mr = Ring(PE, [(7,)])
                wide_ring = Ring(PE, [(k,) for k in range(8)])

                def piece_front(n, m, c, mr=mr):
                    b, jp = pairs_[n]
                    w = n % 2
                    if m == 0:
                        for e in (PE, V, A):
                            e.wait(sels[b][jp].now())
                    k, (bk,) = mr.take()
                    if m >= 16:
                        g = m - 16
                        for q in range(4):
                            t = 4 * g + q
                            last = nc.tensor.matmul(bank(bk)[:, q * P:(q + 1) * P], chans[:, b, PAD + t * P:PAD + (t + 1) * P],
                                                    wv[:, b, 2 * jp:2 * jp + 2, :], start=True, stop=True)
                        p = PE.op(last)
                        V.wait(p, pt.get(("av", n - 2)))
                        for q in range(4):
                            p = V.op(nc.vector.tensor_tensor(vt[:, w, 4 * g + q], bank(bk)[:, q * P:(q + 1) * P].rearrange("p (h x) -> p h x", h=2),
                                                             bv[:, b, 2 * jp:2 * jp + 2, :], ALU.add))
                        mr.release(k, p)
                        pt["vready", n] = p
                        return
                    g, h, kq = m // 4, m // 2 % 2, m % 2
                    j, s = 2 * jp + h, c % 3
                    p = PE.op(nc.tensor.matmul(bank(bk), ws[:, b, kq, j, :, :], chans[:, b, PAD + g * BANK:PAD + (g + 1) * BANK],
                                               start=True, stop=True))
                    A.wait(p, pt.get(("piece_read", c - 3)))
                    p = A.op(nc.scalar.activation(q32[:, s, :], bank(bk), ACT.Identity, bias=bqk[:, b, kq, j:j + 1]))
                    mr.release(k, p)
                    V.wait(p, *pt.get(("parts_read", c - 2), ()))
                    hi = qhh[:, w, h, g * BANK:(g + 1) * BANK] if kq == 0 else parts[:, 0, :]
                    p = V.op(nc.vector.tensor_copy(hi, q32[:, s, :]))
                    e, q_ = (V, nc.vector) if n == 0 else (G, nc.gpsimd)
                    e.wait(p, e.now())
                    pt["rest", c] = e.op(q_.tensor_tensor(q32[:, s, :], q32[:, s, :], hi, ALU.subtract))
                    pt["hi", c] = p

                def piece_back(n, m, c):
                    if m >= 16:
                        return
                    w = n % 2
                    g, h, kq = m // 4, m // 2 % 2, m % 2
                    s = c % 3
                    cs = slice(g * BANK, (g + 1) * BANK)
                    hi = qhh[:, w, h, cs] if kq == 0 else parts[:, 0, :]
                    mid = qmm[:, w, h, cs] if kq == 0 else parts[:, 1, :]
                    A.wait(pt["rest", c])
                    G.wait(pt["rest", c])
                    p = A.op(nc.scalar.copy(mid, q32[:, s, :]))
                    G.wait(p, G.now())
                    V.wait(p)
                    if kq == 0:
                        lo = qhl[64:128, w, h, cs]
                        g1 = G.op(nc.gpsimd.tensor_tensor(lo, q32[64:128, s, :], mid[64:128], ALU.subtract))
                        V.op(nc.vector.tensor_copy(qhl[0:64, w, h, cs], hi[0:64]))
                    else:
                        lo = klh[0:64, w, h, cs]
                        g1 = G.op(nc.gpsimd.tensor_tensor(lo, q32[0:64, s, :], mid[0:64], ALU.subtract))
                        V.op(nc.vector.tensor_copy(khm[0:64, w, h, cs], hi[0:64]))
                        V.op(nc.vector.tensor_copy(khm[64:128, w, h, cs], mid[64:128]))
                        V.op(nc.vector.tensor_copy(klh[64:128, w, h, cs], hi[64:128]))
                    pt["piece_read", c] = g1
                    pt["parts_read", c] = (g1, V.now())
                    pt["qkready", n] = (g1, V.now(), p)

                def scores(u):
                    n, i, h = units[u]
                    w = n % 2
                    qs = slice(i * P, (i + 1) * P)
                    if i == 0 and h == 0:
                        PE.wait(*pt["qkready", n])
                    ks = []
                    for hf in range(2):
                        k, bks = sr.take()
                        for jj in range(2):
                            cs = slice((hf * 2 + jj) * BANK, (hf * 2 + jj + 1) * BANK)
                            nc.tensor.matmul(bank(bks[jj]), qhh[:, w, h, qs], khm[:, w, h, cs], start=True, stop=False)
                            nc.tensor.matmul(bank(bks[jj]), qmm[:, w, h, qs], khm[:, w, h, cs], start=False, stop=False)
                            last = nc.tensor.matmul(bank(bks[jj]), qhl[:, w, h, qs], klh[:, w, h, cs], start=False, stop=True)
                        V.wait(PE.op(last), pt.get(("exp", u - 4)))
                        V.op(nc.vector.tensor_reduce(m2[:, u % 4, hf:hf + 1], psum[:, bks[0]:bks[0] + 2, :].rearrange("p b n -> p (b n)"), X, ALU.max))
                        ks.append((k, bks))
                    V.wait(V.now())
                    pt["max", u] = V.op(nc.vector.tensor_scalar(nm[:, u % 4:u % 4 + 1], m2[:, u % 4, 0:1], m2[:, u % 4, 1:2], -SC, ALU.max, ALU.mult))
                    pt["banks", u] = ks

                def exps(u):
                    A.wait(pt["max", u], pt.get(("turned", u - 2)), pt.get(("rsum", u - 8)))
                    for hf, (k, bks) in enumerate(pt["banks", u]):
                        p = A.op(nc.scalar.activation(pb[:, u % 2, hf * 2 * BANK:(hf + 1) * 2 * BANK],
                                                      psum[:, bks[0]:bks[0] + 2, :].rearrange("p b n -> p (b n)"), ACT.Exp,
                                                      bias=nm[:, u % 4:u % 4 + 1], scale=SC, accum_out=rs[:, u % 8, hf:hf + 1]))
                        sr.release(k, p)
                    pt["exp", u] = p

                def turn(u, g, e):
                    PE.wait(pt["exp", u])
                    k, (bk,) = tr.take()
                    for q in range(4):
                        last = nc.tensor.transpose(bank(bk)[:, q * P:(q + 1) * P], pb[:, u % 2, (4 * g + q) * P:(4 * g + q + 1) * P], ident[:, :])
                    pt["turned", u] = PE.op(last)
                    return k, bk, pt["turned", u]

                def land(u, g, e, t):
                    k, bk, p = t
                    e.wait(p, pt.get(("av_tile", u // 2 - 2)))
                    o = pT[:, u % 4, 4 * g:4 * g + 4, :].rearrange("p q n -> p (q n)")
                    c = A.op(nc.scalar.copy(o, bank(bk))) if e is A else V.op(nc.vector.tensor_copy(o, bank(bk)))
                    tr.release(k, c)
                    pt.setdefault(("pT", u), []).append(c)

                def av(t, half):
                    n, i, _ = units[2 * t]
                    if half == 0:
                        PE.wait(*pt["pT", 2 * t], *pt["pT", 2 * t + 1], pt["vready", n])
                        pt["obank", t] = orr.take()
                    k, (bk,) = pt["obank", t]
                    for kt in range(half * NT // 2, (half + 1) * NT // 2):
                        for h in range(2):
                            last = nc.tensor.matmul(bank(bk)[64 * h:64 * h + 64, 0:P], vt[:, n % 2, kt, h, :], pT[:, (2 * t + h) % 4, kt, :],
                                                    start=(kt == 0), stop=(kt == NT - 1), skip_group_check=True,
                                                    tile_position=(0, 64 * h))
                    if half == 1:
                        pt["av_tile", t] = pt["av", n] = p = PE.op(last)
                        V.wait(p, pt.get(("proj", t - 2)))
                        c = V.op(nc.vector.tensor_copy(oT[:, t % 2, :], bank(bk)[:, 0:P]))
                        orr.release(k, c)
                        pt["oT", t] = c
                        r = rs[:, (2 * t) % 8:(2 * t) % 8 + 2, :]
                        V.wait(pt["exp", 2 * t + 1])
                        V.step(nc.vector.tensor_tensor(r[:, :, 0], r[:, :, 0], r[:, :, 1], ALU.add))
                        pt["recip", t] = V.op(nc.vector.reciprocal(r[:, :, 0], r[:, :, 0]))

                def project(t):
                    n, i, _ = units[2 * t]
                    b, jp = pairs_[n]
                    PE.wait(pt["oT", t])
                    k, (bk,) = mr.take()
                    for h in range(2):
                        PE.wait(PE.now() if h else None)
                        pt["proj", t] = PE.op(nc.tensor.matmul(bank(bk)[:, h * D:(h + 1) * D], oT[64 * h:64 * h + 64, t % 2, :],
                                                               wo[64 * h:64 * h + 64, jp, :], start=True, stop=True))
                    x = res[:, b * NT + i, :]
                    V.wait(pt["proj", t], pt["recip", t], pt["bias", b])
                    for h in range(2):
                        p = V.step(nc.vector.scalar_tensor_tensor(x, bank(bk)[:, h * D:(h + 1) * D], rs[:, (2 * t + h) % 8, 0:1], x, ALU.mult, ALU.add))
                    mr.release(k, p)
                    pt["rsum", 2 * t] = pt["rsum", 2 * t + 1] = p

                NPIECE = 20
                beside = [iter(()) for _ in pairs_]
                for b in range(1, NB):
                    beside[(b - 1) * NPAIR] = choose(b, mr)
                for e in (A, V):
                    e.wait(*pt["norm_free"])
                for m in range(NPIECE):
                    piece_front(0, m, m, wide_ring)
                    if m:
                        piece_back(0, m - 1, m - 1)
                PE.wait(V.now(), A.now())
                scores(0)
                exps(0)
                for u in range(NU + 3):
                    if u + 1 < NU:
                        scores(u + 1)
                    n, i, h = units[min(u, NU - 1)]
                    m, c = 2 * i + h, NPIECE * (n + 1) + 2 * i + h
                    pieces = u < NU and n + 1 < len(pairs_)
                    if pieces and m < NPIECE:
                        piece_front(n + 1, m, c)
                    ts = {}
                    if u < NU:
                        ts[0] = turn(u, 0, A)
                        land(u, 0, A, ts[0])
                        ts[1] = turn(u, 1, A)
                        land(u, 1, A, ts[1])
                    t, half = (u - 2) // 2, (u - 2) % 2
                    if u >= 2 and 2 * t < NU:
                        av(t, half)
                    if u < NU:
                        for g in (2, 3):
                            land(u, g, V, turn(u, g, V))
                    if u + 1 < NU:
                        exps(u + 1)
                    if u >= 4 and u % 2 == 0:
                        project((u - 4) // 2)
                    if pieces:
                        if 1 <= m <= NPIECE:
                            piece_back(n + 1, m - 1, c - 1)
                        if m == NPIECE + 1:
                            V.wait(A.now(), G.now())
                        if m > NPIECE:
                            for _ in range(5):
                                next(beside[n], None)
                        if m == 2 * NT - 1:
                            for _ in beside[n]:
                                pass
                            for e in (A, V):
                                e.wait(*pt["norm_free"])
                barrier()

        def phase_F():
            HID = a["W_q"].shape[1]
            with ExitStack() as st:
                w = sb(st, "d_w", [P, 3 * HID])
                bias = sb(st, "d_b", [P, 3, HID])
                wo = sb(st, "d_wo", [P, HID])
                bo = sb(st, "d_bo", [P, HID])
                ld = new_loads("diag_loads")
                for n, name in enumerate(("q", "k", "v")):
                    ld.start(w[:, n * HID:(n + 1) * HID], a["W_" + name])
                    ld.start(bias[:, n, :], bcast(a["b_" + name], P))
                ld.start(wo[:, :], a["W_o"])
                ld.start(bo[:, :], bcast(a["b_o"], P))
                qf = sb(st, "d_qk", [P, 2, 2 * HID])
                vf = sb(st, "d_v", [P, 3, HID])
                rest = sb(st, "d_rest", [P, 2 * HID])
                part = sb(st, "d_parts", [P, 3, 2 * HID], BF16)
                uq = sb(st, "d_q_rows", [P, 2, NH, ROWS], BF16)
                uk = sb(st, "d_k_rows", [P, 2, NH, ROWS], BF16)
                qT = sb(st, "d_qT", [ROWS, 2, NH * P], BF16)
                kT = sb(st, "d_kT", [ROWS, 2, NH * P], BF16)
                dg = sb(st, "d_diag", [P, 3, NH])
                dj = sb(st, "d_diag_terms", [P, HID])
                mh = sb(st, "d_negmax", [P, 2, NH, 2])
                sh = sb(st, "d_sums", [P, 2, NH, 2])
                mm = sb(st, "d_negmax_all", [P, NH])
                cf = sb(st, "d_coeff", [P, NH, 2])
                junk = sb(st, "d_junk", [P, 3, 2 * BANK], BF16)
                junked = []
                ov = sb(st, "d_out", [P, HID])
                oT = sb(st, "d_oT", [P, HID])
                first_norm = layernorm(res, norm[:, :, :], 0, 1e-5)
                for e in (PE, V, A, G):
                    e.wait(ld.now())
                G.op(nc.gpsimd.memset(uq[:, :, :, NG * HD:ROWS], 0.0))
                G.op(nc.gpsimd.memset(uk[:, :, :, NG * HD:ROWS], 0.0))
                SCALE = float(1.0 / np.sqrt(np.float32(HID)))
                V.op(nc.vector.tensor_scalar(w[:, 0:2 * HID], w[:, 0:2 * HID], SCALE, None, ALU.mult))
                V.op(nc.vector.tensor_scalar(bias[:, 0:2, :], bias[:, 0:2, :], SCALE, None, ALU.mult))
                for b in range(NB):
                    ring = Ring(PE, [(k,) for k in range(8)])
                    done = to_channels(ring, norm, layernorm(res, norm[:, :, :], b, 1e-5) if b else first_norm, b)
                    V.wait(*done)
                barrier()
                V.op(nc.vector.tensor_tensor(res[:, :, :], res[:, :, :], wide(bo[:, :].rearrange("p (o n) -> p o n", o=1), 1, R), ALU.add))
                tr = Ring(PE, [(0,), (1,)])
                sr = Ring(PE, [(2, 3), (4, 5), (6, 7)])
                pt = {}

                def prep(T):
                    b, i, s = T // NT, T % NT, T % 2
                    k, (bk,) = tr.take()
                    p = PE.op(nc.tensor.matmul(bank(bk)[:, 0:3 * HID], chans[:, b, PAD + i * P:PAD + (i + 1) * P], w[:, :], start=True, stop=True))
                    yield
                    V.wait(p, pt.get(("rest", T - 1)), pt.get(("terms", T - 1)), pt.get(("closed", T - 3)))
                    V.op(nc.vector.tensor_tensor(qf[:, s, :], bank(bk)[:, 0:2 * HID], bias[:, 0:2, :].rearrange("p n h -> p (n h)"), ALU.add))
                    p = V.op(nc.vector.tensor_tensor(vf[:, T % 3, :], bank(bk)[:, 2 * HID:3 * HID], bias[:, 2, :], ALU.add))
                    tr.release(k, p)
                    V.wait(p, pt.get(("spread", T - 1)))
                    hi = V.op(nc.vector.tensor_copy(part[:, 0, :], qf[:, s, :]))
                    G.wait(p, pt.get(("diag", T - 1)), G.now())
                    pt["terms", T] = G.op(nc.gpsimd.tensor_tensor(dj[:, :], qf[:, s, 0:HID], qf[:, s, HID:2 * HID], ALU.mult))
                    G.wait(hi, G.now())
                    r = G.op(nc.gpsimd.tensor_tensor(rest[:, :], qf[:, s, :], part[:, 0, :], ALU.subtract))
                    yield
                    yield
                    V.wait(r, pt.get(("closed", T - 3)))
                    mid = V.op(nc.vector.tensor_copy(part[:, 1, :], rest[:, :]))
                    pt["diag", T] = V.op(nc.vector.tensor_reduce(dg[:, T % 3, :], dj[:, :].rearrange("p (h x) -> p h x", x=HD), X, ALU.add))
                    G.wait(mid, G.now())
                    lo = G.op(nc.gpsimd.tensor_tensor(part[:, 2, :], rest[:, :], part[:, 1, :], ALU.subtract))
                    pt["rest", T] = lo
                    yield
                    yield
                    V.wait(lo, pt.get(("turned", T - 2)))
                    G.wait(pt.get(("turned", T - 2)))
                    qr = uq[:, s, :, 0:NG * HD].rearrange("p h (i j x) -> p h i j x", i=3, j=3)
                    kr = uk[:, s, :, 0:NG * HD].rearrange("p h (i j x) -> p h i j x", i=3, j=3)
                    for g in range(3):
                        for c in range(3):
                            V.op(nc.vector.tensor_copy(qr[:, :, g, c, :], part[:, g, 0:HID].rearrange("p (h x) -> p h x", x=HD)))
                        for c in range(3):
                            G.wait(G.now())
                            G.op(nc.gpsimd.tensor_copy(kr[:, :, c, g, :], part[:, g, HID:2 * HID].rearrange("p (h x) -> p h x", x=HD)))
                        yield
                    pt["spread", T] = G.now()
                    spread_q = V.now()
                    yield
                    PE.wait(spread_q)
                    for u, dst in ((uq, qT), (uk, kT)):
                        for g in range(2):
                            if u is uk and g == 0:
                                PE.wait(pt["spread", T])
                            k, (bk,) = tr.take()
                            bvw = psum[0:ROWS, bk, :].bitcast(BF16)
                            for q in range(8):
                                p = nc.tensor.transpose(bvw[:, q * P:(q + 1) * P], u[:, s, 8 * g + q, :], identb[:, :])
                                if q == 7:
                                    p = PE.op(p)
                                if q % 3 == 2:
                                    yield
                            if u is uq and g == 0:
                                V.wait(p, pt.get(("scored", T - 2)))
                                c = V.op(nc.vector.tensor_copy(dst[:, s, g * 8 * P:(g + 1) * 8 * P], bvw))
                                pt["rows0", T] = c
                            else:
                                A.wait(p, pt.get(("scored", T - 2)))
                                c = A.op(nc.scalar.copy(dst[:, s, g * 8 * P:(g + 1) * 8 * P], bvw))
                            tr.release(k, c)
                    pt["turned", T] = p
                    pt["rows", T] = c

                def score(T, jb, hf):
                    s = T % 2
                    k, bks = sr.take()
                    for jj in range(2):
                        c = hf * 2 + jj
                        last = nc.tensor.matmul(bank(bks[jj]), kT[:, s, jb * P:(jb + 1) * P], qT[:, s, c * BANK:(c + 1) * BANK], start=True, stop=True)
                    blk = psum[:, bks[0]:bks[0] + 2, :].rearrange("p b n -> p (b n)")
                    pt["scored", T] = PE.op(last)
                    V.wait(pt["scored", T])
                    p = V.op(nc.vector.tensor_reduce(mh[:, s, jb, hf:hf + 1], blk, X, ALU.max, negate=True))
                    A.wait(p, junked[-3] if len(junked) > 2 else None)
                    p = A.op(nc.scalar.activation(junk[:, len(junked) % 3, :], blk, ACT.Exp, bias=mh[:, s, jb, hf:hf + 1],
                                                  accum_out=sh[:, s, jb, hf:hf + 1]))
                    junked.append(p)
                    sr.release(k, p)
                    pt["summed", T] = p

                def close(T):
                    s = T % 2
                    V.wait(pt["summed", T])
                    V.step(nc.vector.tensor_tensor(mm[:, :], mh[:, s, :, 0], mh[:, s, :, 1], ALU.min))
                    for hf in range(2):
                        V.op(nc.vector.tensor_tensor(cf[:, :, hf], mm[:, :], mh[:, s, :, hf], ALU.subtract))
                    d3 = dg[:, T % 3, :]
                    p = V.op(nc.vector.tensor_tensor(d3, d3, mm[:, :], ALU.add))
                    yield
                    A.wait(p)
                    A.op(nc.scalar.activation(cf[:, :, :], cf[:, :, :], ACT.Exp))
                    p = A.op(nc.scalar.activation(d3, d3, ACT.Exp))
                    yield
                    V.wait(p)
                    V.step(nc.vector.tensor_tensor(cf[:, :, :], cf[:, :, :], sh[:, s, :, :], ALU.mult))
                    V.step(nc.vector.tensor_tensor(mm[:, :], cf[:, :, 0], cf[:, :, 1], ALU.add))
                    V.step(nc.vector.reciprocal(mm[:, :], mm[:, :]))
                    V.step(nc.vector.tensor_tensor(mm[:, :], mm[:, :], d3, ALU.mult))
                    p = V.op(nc.vector.tensor_tensor(ov[:, :].rearrange("p (h x) -> p h x", x=HD), vf[:, T % 3, :].rearrange("p (h x) -> p h x", x=HD),
                                                     wide(mm[:, :].rearrange("p (h o) -> p h o", o=1), 2, HD), ALU.mult))
                    pt["closed", T] = p
                    yield
                    yield
                    PE.wait(p)
                    k, (bk,) = tr.take()
                    p = PE.op(nc.tensor.transpose(bank(bk)[:, 0:P], ov[:, :], ident[:, :]))
                    yield
                    V.wait(p)
                    c = V.op(nc.vector.tensor_copy(oT[:, :], bank(bk)[:, 0:P]))
                    tr.release(k, c)
                    yield
                    yield
                    PE.wait(c)
                    k, (bk,) = tr.take()
                    p = PE.op(nc.tensor.matmul(bank(bk)[:, 0:D], oT[:, :], wo[:, :], start=True, stop=True))
                    yield
                    V.wait(p)
                    x = res[:, T, :]
                    c = V.op(nc.vector.tensor_tensor(x, x, bank(bk)[:, 0:D], ALU.add))
                    tr.release(k, c)

                for _ in prep(0):
                    pass
                for T in range(R):
                    PE.wait(pt["rows", T], pt["rows0", T])
                    side = []
                    if T >= 1:
                        side.append(close(T - 1))
                    if T + 1 < R:
                        side.append(prep(T + 1))
                    for jb in range(NH):
                        for hf in range(2):
                            score(T, jb, hf)
                            for g in reversed(side):
                                next(g, None)
                    for g in side:
                        for _ in g:
                            pass
                for _ in close(R - 1):
                    pass
                barrier()

        run = {"H": phase_H, "M": phase_M, "T": phase_T, "C": phase_C, "D": phase_D,
               "E": lambda: phase_E("_1"), "F": phase_F, "E2": lambda: phase_E("_2")}
        for ph in phases:
            run[ph]()
        store = new_loads("store")
        barrier()
        store.start(out.rearrange("b (i p) d -> p (b i) d", p=P), res[:, :, :])
        SP.wait(store.now())


def kernel(**inputs):
    import concourse.bacc as bacc
    from concourse.bass_utils import run_bass_kernel_spmd

    nc = bacc.Bacc("TRN2", target_bir_lowering=False, num_devices=1)
    arrays, aps = {}, {}
    for name, value in {**inputs, **constants()}.items():
        short = name.replace("L0_attn_a_", "").replace("L0_attn_b_", "").replace("L0_ffn_", "")
        v = np.ascontiguousarray(value)
        if v.ndim == 0:
            v = v.reshape(1)
        arrays["in_" + short] = v
        aps[short] = nc.dram_tensor("in_" + short, v.shape, mybir.dt.from_np(v.dtype), kind="ExternalInput").ap()
    shape = inputs["L0_attn_a_hidden_states"].shape
    out = nc.dram_tensor("out", shape, F32, kind="ExternalOutput").ap()
    build(nc, aps, out, shape)
    r = run_bass_kernel_spmd(nc, [arrays], core_ids=[0])
    return r.results[0]["out"]
```
